# Optimizing a Trainium2 kernel written in Bass

```python
import numpy as np
import jax
import jax.numpy as jnp

def _softmax(x, axis=-1):
    return jax.nn.softmax(x, axis=axis)

def _gelu(x):
    return jax.nn.gelu(x, approximate=True)

def _silu(x):
    return jax.nn.silu(x)

def _sigmoid(x):
    return jax.nn.sigmoid(x)

def _layernorm(x, axis=-1, eps=1e-05):
    m = jnp.mean(x, axis=axis, keepdims=True)
    v = jnp.var(x, axis=axis, keepdims=True)
    return (x - m) / jnp.sqrt(v + eps)

def _scatter_add(tgt, idx, src, axis=0):
    return tgt.at[idx].add(src)

def _segment_sum(src, seg, n):
    return jax.ops.segment_sum(src, seg, n)
kernel_name = 'mk_flamingo_gated_d1_seqx_r4_c3582e'

def setup_inputs(seed: int=0):
    np.random.seed(seed)
    _w = jnp.asarray

    def _rec_inputs():
        import jax
        import jax.numpy as jnp
        _rk = jax.random.key(seed)
        x = 7.22e-05 + 1 * jax.random.normal(jax.random.fold_in(_rk, 1), (16, 256, 512), jnp.float32)
        _lenS = 256 - jax.random.randint(jax.random.fold_in(_rk, 7), (16,), 0, max(1, 256 // 4) + 1, jnp.int32)
        _lenS2 = 256 - jax.random.randint(jax.random.fold_in(_rk, 8), (16,), 0, max(1, 256 // 4) + 1, jnp.int32)
        _ctx_1024P = jax.random.normal(jax.random.fold_in(_rk, 11), (16, 16, 256), jnp.float32)
        _ctx_1024c = jax.random.dirichlet(jax.random.fold_in(_rk, 511), 0.3 * jnp.ones((16,), jnp.float32), (16, 256))
        _ctx_1024t = jnp.einsum('bsk,bkd->bsd', _ctx_1024c, _ctx_1024P)
        _ctx_1024t = _ctx_1024t * jax.lax.rsqrt(jnp.mean(jnp.square(_ctx_1024t)) + 1e-12) * 0.953939
        ctx_1024 = -1.39393e-06 + 0.999914 * (_ctx_1024t + 0.3 * jax.random.normal(jax.random.fold_in(_rk, 611), (16, 256, 256), jnp.float32))
        fside_BxSx2_0 = jax.random.uniform(jax.random.fold_in(_rk, 12), (16, 256, 2), jnp.float32, 0.0, 0.999707)
        _g = jax.random.normal(jax.random.fold_in(_rk, 9001), (2, 1), jnp.float32)
        _g = jnp.sign(_g) * jnp.maximum(jnp.abs(_g), 1.0) + (_g == 0) * 1.0
        g_xattn = _g[0]
        g_ffn = _g[1]
        return (x, ctx_1024, fside_BxSx2_0, g_xattn, g_ffn)
    x, ctx_1024, fside_BxSx2_0, g_xattn, g_ffn = _rec_inputs()

    def _L0_xattn_setup():
        import jax, jax.numpy as jnp
        import numpy as np
        DIM = 512
        CTX_DIM = 256
        N_HEADS = 32
        HEAD_DIM = DIM // N_HEADS
        POS_DIM = 2
        B, N, CTXN = (2, 512, 512)
        ROPE_BASE = 10000.0

        def apply_axial_rope(x, pos):
            b, n, h, d = x.shape
            p = pos.shape[-1]
            dpa = d // p
            half = dpa // 2
            freqs = ROPE_BASE ** (-jnp.arange(half, dtype=x.dtype) / half)
            ang = pos[..., :, None] * freqs
            cos = jnp.cos(ang)[:, :, None, :, :]
            sin = jnp.sin(ang)[:, :, None, :, :]
            xr = x.reshape(b, n, h, p, half, 2)
            x1, x2 = (xr[..., 0], xr[..., 1])
            out = jnp.stack([x1 * cos - x2 * sin, x1 * sin + x2 * cos], axis=-1)
            return out.reshape(b, n, h, d)
        key = jax.random.key(seed)
        ks = jax.random.split(key, 8)
        x = jax.random.normal(ks[0], (B, N, DIM), jnp.float32)
        ctx = jax.random.normal(ks[1], (B, CTXN, CTX_DIM), jnp.float32)
        pos_map = jax.random.uniform(ks[2], (B, N, POS_DIM), jnp.float32)
        ctx_pos_map = jax.random.uniform(ks[3], (B, CTXN, POS_DIM), jnp.float32)
        Wq = jax.random.normal(ks[4], (DIM, DIM), jnp.float32) / np.sqrt(DIM)
        Wkv = jax.random.normal(ks[5], (CTX_DIM, 2 * DIM), jnp.float32) / np.sqrt(CTX_DIM)
        Wout = jax.random.normal(ks[6], (DIM, DIM), jnp.float32) / np.sqrt(DIM)
        bout = jnp.zeros((DIM,), jnp.float32)
        return {'x': x, 'ctx': ctx, 'pos_map': pos_map, 'ctx_pos_map': ctx_pos_map, 'Wq': Wq, 'Wkv': Wkv, 'Wout': Wout, 'bout': bout}
    _L0_xattn_all = _L0_xattn_setup()
    _L0_xattn_in = {k: v for k, v in _L0_xattn_all.items() if k in ('Wq', 'Wkv', 'Wout', 'bout')}
    del _L0_xattn_all

    def _L0_ffn_setup():
        import jax, jax.numpy as jnp
        import numpy as np
        HID = 512
        INTER = 2048
        NEXP = 8
        TOPK = 2
        EPS = 1e-05

        def _mock_fused_moe(x, selected_experts, routing_weights, expert_weight):
            y = jnp.einsum('bsh,hd->bsd', x, expert_weight)
            scale = routing_weights.sum(axis=-1, keepdims=True)
            return y * scale
        key = jax.random.key(seed)
        ks = jax.random.split(key, 6)
        s = lambda fan_in: 1.0 / np.sqrt(fan_in)
        return {'hidden_states': jax.random.normal(ks[0], (4, 1024, HID), dtype=jnp.float32), 'gate_w': jax.random.uniform(ks[1], (HID, NEXP), jnp.float32, -s(HID), s(HID)), 'up_w': jax.random.uniform(ks[2], (HID, INTER), jnp.float32, -s(HID), s(HID)), 'down_w': jax.random.uniform(ks[3], (INTER, HID), jnp.float32, -s(INTER), s(INTER)), 'expert_weight': jax.random.normal(ks[4], (HID, HID), dtype=jnp.float32), 'ln_gamma': jnp.ones((HID,), jnp.float32), 'ln_beta': jnp.zeros((HID,), jnp.float32)}
    _L0_ffn_all = _L0_ffn_setup()
    _L0_ffn_in = {k: v for k, v in _L0_ffn_all.items() if k in ('gate_w', 'up_w', 'down_w', 'expert_weight', 'ln_gamma', 'ln_beta')}
    del _L0_ffn_all
    return {'x': x, 'ctx_1024': ctx_1024, 'fside_BxSx2_0': fside_BxSx2_0, 'g_xattn': g_xattn, 'g_ffn': g_ffn, 'L0_xattn_Wq': _L0_xattn_in['Wq'], 'L0_xattn_Wkv': _L0_xattn_in['Wkv'], 'L0_xattn_Wout': _L0_xattn_in['Wout'], 'L0_xattn_bout': _L0_xattn_in['bout'], 'L0_ffn_gate_w': _L0_ffn_in['gate_w'], 'L0_ffn_up_w': _L0_ffn_in['up_w'], 'L0_ffn_down_w': _L0_ffn_in['down_w'], 'L0_ffn_expert_weight': _L0_ffn_in['expert_weight'], 'L0_ffn_ln_gamma': _L0_ffn_in['ln_gamma'], 'L0_ffn_ln_beta': _L0_ffn_in['ln_beta']}

def reference(x, ctx_1024, fside_BxSx2_0, g_xattn, g_ffn, L0_xattn_Wq, L0_xattn_Wkv, L0_xattn_Wout, L0_xattn_bout, L0_ffn_gate_w, L0_ffn_up_w, L0_ffn_down_w, L0_ffn_expert_weight, L0_ffn_ln_gamma, L0_ffn_ln_beta):
    import jax
    import jax.numpy as jnp

    def _L0_xattn_ref(x, ctx, pos_map, ctx_pos_map, Wq, Wkv, Wout, bout):
        import jax, jax.numpy as jnp
        import numpy as np
        DIM = 512
        CTX_DIM = 256
        N_HEADS = 32
        HEAD_DIM = DIM // N_HEADS
        POS_DIM = 2
        B, N, CTXN = (2, 512, 512)
        ROPE_BASE = 10000.0

        def apply_axial_rope(x, pos):
            b, n, h, d = x.shape
            p = pos.shape[-1]
            dpa = d // p
            half = dpa // 2
            freqs = ROPE_BASE ** (-jnp.arange(half, dtype=x.dtype) / half)
            ang = pos[..., :, None] * freqs
            cos = jnp.cos(ang)[:, :, None, :, :]
            sin = jnp.sin(ang)[:, :, None, :, :]
            xr = x.reshape(b, n, h, p, half, 2)
            x1, x2 = (xr[..., 0], xr[..., 1])
            out = jnp.stack([x1 * cos - x2 * sin, x1 * sin + x2 * cos], axis=-1)
            return out.reshape(b, n, h, d)
        b, n, _ = x.shape
        ctx_n = ctx.shape[1]
        q = (x @ Wq).reshape(b, n, N_HEADS, HEAD_DIM)
        k, v = jnp.split(ctx @ Wkv, 2, axis=-1)
        k = k.reshape(b, ctx_n, N_HEADS, HEAD_DIM)
        v = v.reshape(b, ctx_n, N_HEADS, HEAD_DIM)
        q = apply_axial_rope(q, pos_map)
        k = apply_axial_rope(k, ctx_pos_map)
        scale = 1.0 / np.sqrt(HEAD_DIM).astype(np.float32)
        logits = jnp.einsum('bqhd,bkhd->bhqk', q, k) * scale
        w = jax.nn.softmax(logits, axis=-1)
        attn = jnp.einsum('bhqk,bkhd->bqhd', w, v)
        attn = attn.reshape(b, n, N_HEADS * HEAD_DIM)
        return attn @ Wout + bout

    def _L0_ffn_ref(hidden_states, gate_w, up_w, down_w, expert_weight, ln_gamma, ln_beta):
        import jax, jax.numpy as jnp
        import numpy as np
        HID = 512
        INTER = 2048
        NEXP = 8
        TOPK = 2
        EPS = 1e-05

        def _mock_fused_moe(x, selected_experts, routing_weights, expert_weight):
            y = jnp.einsum('bsh,hd->bsd', x, expert_weight)
            scale = routing_weights.sum(axis=-1, keepdims=True)
            return y * scale
        residuals = hidden_states
        logits = jnp.einsum('bsh,he->bse', hidden_states, gate_w)
        routing_weights, selected_experts = jax.lax.top_k(logits, TOPK)
        h = jnp.einsum('bsh,hi->bsi', residuals, up_w)
        h = jnp.square(jax.nn.relu(h))
        shared_out = jnp.einsum('bsi,ih->bsh', h, down_w)
        moe_out = _mock_fused_moe(hidden_states, selected_experts, routing_weights, expert_weight)
        y = shared_out + moe_out
        mu = y.mean(axis=-1, keepdims=True)
        var = jnp.mean(jnp.square(y - mu), axis=-1, keepdims=True)
        return (y - mu) * jax.lax.rsqrt(var + EPS) * ln_gamma + ln_beta
    x = x + jnp.tanh(g_xattn[0]) * _L0_xattn_ref(_layernorm(x, axis=-1), ctx_1024, fside_BxSx2_0, fside_BxSx2_0, L0_xattn_Wq, L0_xattn_Wkv, L0_xattn_Wout, L0_xattn_bout)
    x = x + jnp.tanh(g_ffn[0]) * _L0_ffn_ref(_layernorm(x, axis=-1), L0_ffn_gate_w, L0_ffn_up_w, L0_ffn_down_w, L0_ffn_expert_weight, L0_ffn_ln_gamma, L0_ffn_ln_beta)
    return x

_drawn_inputs = setup_inputs


def setup_inputs(seed=0):
    import zlib

    import numpy as np

    out = dict(_drawn_inputs(seed))
    spreads = {'L0_xattn_bout': (0.0, 0.1), 'L0_ffn_ln_gamma': (1.0, 0.2), 'L0_ffn_ln_beta': (0.0, 0.1)}
    factors = {'L0_ffn_up_w': 4.249, 'L0_ffn_down_w': 3.873}
    for name, (base, spread) in spreads.items():
        noise = np.random.default_rng([zlib.crc32(name.encode()), seed]).standard_normal(out[name].shape)
        drawn = base * np.exp(spread * noise) if base else spread * noise
        out[name] = jnp.asarray(drawn.astype(out[name].dtype))
    for name, factor in factors.items():
        out[name] = (out[name] * factor).astype(out[name].dtype)
    return out
```

```python
from contextlib import ExitStack

import numpy as np

import concourse.bass as bass
from concourse import mybir
from concourse.alu_op_type import AluOpType as ALU

F32 = mybir.dt.float32
F32R = mybir.dt.float32r
ACT = mybir.ActivationFunctionType
AX = mybir.AxisListType

P = 128
B, S, D = 16, 256, 512
CD = 256
NH, HD = 32, 16
INTER, NEXP = 2048, 8
EPS = 1e-5
ROPE_BASE = 10000.0
POS = 2
HALF = HD // POS // 2
ANG = POS * HALF
TT = S // P
KC = D // P
CC = CD // P
NT = B * TT
STEPS = NH // 2
GROUPS = NH // 4
SCALE = 1.0 / float(np.sqrt(HD))
MC = INTER // P
BLK = 512
NB = B * S // BLK
UT = BLK // P
INC = 16

Q_PARTS = (0, 1, 0)
K_PARTS = (0, 0, 1)
ROWS_A = 3 * HD
ROWS_B = ROWS_A + 2
STACK_DMAS = 2 * len(Q_PARTS) * 2
PASSES = ((0, 0), (1, 0), (0, 1))

PREP_JOBS = ("K0", "X0", "Q0", "kT0", "qT0", "X1", "Q1", "K1", "qT1", "kT1")
PREP_SPLITS = tuple(job for job in PREP_JOBS if job[0] == "X" or job[1] == "T")
ROPES = tuple(job for job in PREP_JOBS if job[0] in "QK")
MID_JOBS = ("m0", "V0", "V1", "m1")
V_DONE = MID_JOBS.index("V1") + 1
POOL_ORDER = (0, "K0", "Q0", 1, "Q1", "K1")
TAIL_JOBS = ("a00", "a10", "a01", "a11", "aT0", "O0", "aT1", "O1")
LN_AT = (0, 5)

SLOTS = {
    (0, 1): ["p:K0"], (1, 0): ["t:a01"], (1, 1): ["p:X0"], (2, 0): ["t:a11"], (2, 1): ["p:Q0<"],
    (3, 0): ["n:m1"], (3, 1): ["p:Q0"], (4, 0): ["t:aT0"], (4, 1): ["p:kT0"], (5, 0): ["p:qT0"],
    (5, 1): ["t:O0<"], (6, 0): ["p:X1"], (6, 1): ["t:O0"], (7, 1): ["p:Q1<"], (8, 0): ["t:aT1"],
    (8, 1): ["p:Q1"], (9, 0): ["m:m0"], (9, 1): ["p:K1"], (10, 0): ["p:qT1"], (10, 1): ["t:O1<"],
    (11, 0): ["p:kT1"], (11, 1): ["t:O1"], (12, 1): ["m:V0"], (13, 0): ["h:a00"], (13, 1): ["m:V1"],
    (14, 0): ["h:a10"],
}


def jobs_of(kinds):
    return [(x[0], x[2:]) for at in sorted(SLOTS) for x in SLOTS[at] if x[0] in kinds and x[-1] != "<"]


assert [x for _, x in jobs_of("p")] == list(PREP_JOBS)
assert jobs_of("th") == [("t", x) for x in TAIL_JOBS[2:]] + [("h", x) for x in TAIL_JOBS[:2]]
assert jobs_of("mn") == [("n", MID_JOBS[-1])] + [("m", x) for x in MID_JOBS[:-1]]


CUT = [x[2:-1] for items in SLOTS.values() for x in items if x[-1] == "<"]


def some(count):
    return not isinstance(count, int) or count > 0


def within(b):
    return not isinstance(b, int) or 0 <= b < B


def flamingo_gated(nc, x, ctxT, posT, g_x, g_f, wq, wkv, wout, bout, gate, up, down, wexp, gamma, beta, out):
    xt_d = x.rearrange("b (t p) d -> (b t) p d", p=P)
    out_d = out.rearrange("b (t p) d -> (b t) p d", p=P)
    ctx_d = ctxT.rearrange("b (c p) s -> b p c s", p=P)
    qk_d = [[nc.dram_tensor(f"{x}T_scratch{par}", [2, D, S], F32, kind="Internal").ap() for x in "qk"]
            for par in range(2)]
    x1_d = nc.dram_tensor("x1_scratch", [NT, P, D], F32, kind="Internal").ap()

    with ExitStack() as stack:
        def sem(name):
            return stack.enter_context(nc.semaphore(name))

        def bank(name, shape):
            return stack.enter_context(nc.psum_tensor(name, shape, F32))

        pA = bank("pA", [P, 2, 512])
        pB = bank("pB", [P, 2, 512])
        pO = bank("pO", [P, 512])
        pP = bank("pP", [P, 512])
        pM = bank("pM", [P, 512])
        pT = bank("pT", [P, 512])
        acc = [pA[:, 0, :], pA[:, 1, :], pB[:, 0, :], pB[:, 1, :]]
        pU = [pO[:, :], pP[:, :]]
        pE = pM[:, :]
        pX = pT[:, :]

        def keep(name, shape, dt=F32):
            return stack.enter_context(nc.sbuf_tensor(name, shape, dt))

        ident = keep("ident", [P, P])
        g_att = keep("g_att", [P, 1])
        g_ffn = keep("g_ffn", [P, 1])
        neg_half = keep("neg_half", [P, 1])
        stats = keep("stats", [P, 6])
        meanvar = keep("meanvar", [P, 2])
        var_eps = keep("var_eps", [P, 1])
        rstd = keep("rstd", [P, 1])

        first = ExitStack()

        def sb1(name, shape, dt=F32):
            return first.enter_context(nc.sbuf_tensor(name, shape, dt))

        wq_s = [sb1(f"wq{i}", [P, KC, D], F32R) for i in range(2)]
        wk_s = [sb1(f"wk{i}", [P, CC, D], F32R) for i in range(2)]
        wv_s = [sb1(f"wv{i}", [P, CC, D], F32R) for i in range(2)]
        wo_s = [sb1(f"wo{i}", [P, KC, D], F32R) for i in range(2)]
        st_q = [sb1(f"stq{i}", [P, STEPS, S], F32R) for i in range(2)]
        st_k = [sb1(f"stk{i}", [P, STEPS, S], F32R) for i in range(2)]
        qT = [sb1(f"qT{i}", [P, KC, S], F32R) for i in range(2)]
        kT = [sb1(f"kT{i}", [P, KC, S], F32R) for i in range(2)]
        probs = sb1("probs", [P, 4, 2, TT, S])
        v_s = [sb1(f"v{i}", [P, TT, NH, HD + 1]) for i in range(2)]
        ctx_raw = sb1("ctx_raw", [P, CC, S])
        ctx_s = [[sb1(f"ctx{i}{j}", [P, CC, S], F32R) for j in range(2)] for i in range(2)]
        xin = [sb1(f"xin{i}", [P, D]) for i in range(2)]
        xn = sb1("xn", [P, D])
        xnT = [sb1(f"xnT{i}", [P, KC, P], F32R) for i in range(2)]
        rot = {"Q": sb1("rot_q", [P, D]), "K": sb1("rot_k", [P, D])}
        rot2 = sb1("rot2", [P, D])
        cos_t = sb1("cos_t", [P, NT, ANG, 2])
        sin_t = sb1("sin_t", [P, NT, ANG, 2])
        av_s = sb1("av_s", [P, GROUPS, S])
        attn = [sb1(f"attn{t}", [P, D]) for t in range(TT)]
        rden = sb1("rden", [P, NH // 2])
        aT = [sb1(f"aT{i}", [P, KC, P], F32R) for i in range(2)]
        xres = [sb1(f"xres{i}", [P, D]) for i in range(2)]
        gbout = sb1("gbout", [P, D])
        mneg = [sb1(f"mneg{i}", [P, TT, NH]) for i in range(2)]
        mT = [sb1(f"mT{i}", [NH // 2, S], F32R) for i in range(2)]

        raw1 = [probs[:, k, :, :, :].rearrange("p a b s -> p (a b s)")[:, 0:D] for k in range(4)]
        pos_s = av_s[:, 0, 0:NT * POS].rearrange("p (n a) -> p n a", a=POS)
        ang = av_s[:, 1, 0:NT * ANG].rearrange("p (n a j) -> p n a j", a=POS, j=HALF)
        turns = av_s[:, 2, 0:NT * ANG].rearrange("p (n a j) -> p n a j", a=POS, j=HALF)
        sin_a = av_s[:, 3, 0:NT * ANG].rearrange("p (n k) -> p n k", k=ANG)
        cos_a = av_s[:, 4, 0:NT * ANG].rearrange("p (n k) -> p n k", k=ANG)
        first.close()

        second = ExitStack()

        def sb2(name, shape, dt=F32):
            return second.enter_context(nc.sbuf_tensor(name, shape, dt))

        up_s = [sb2(f"up{i}", [P, KC, INTER], F32R) for i in range(2)]
        dn_s = [sb2(f"dn{i}", [P, MC, D], F32R) for i in range(2)]
        ex_s = [sb2(f"ex{i}", [P, KC, D], F32R) for i in range(2)]
        gt_s = [sb2(f"gt{i}", [P, KC, NEXP], F32R) for i in range(2)]
        gt_raw = sb2("gt_raw", [P, KC, NEXP])
        fT = [[sb2(f"fT{i}{j}", [P, KC, BLK], F32R) for j in range(2)] for i in range(2)]
        relu = [sb2(f"relu{i}", [P, BLK]) for i in range(2)]
        hid = [[sb2(f"hid{i}{j}", [P, BLK], F32R) for j in range(2)] for i in range(2)]
        fx = sb2("fx", [P, D])
        fres = sb2("fres", [P, D])
        y_s = sb2("y_s", [P, UT, D])
        g_gamma = sb2("g_gamma", [P, D])
        g_beta = sb2("g_beta", [P, D])
        gl = sb2("gl", [NEXP, BLK])
        glT = sb2("glT", [P, UT, NEXP])
        top = sb2("top", [P, UT, 8])
        route = [sb2(f"route{i}", [P, UT]) for i in range(2)]
        second.close()

        ident_made = sem("ident_made")
        consts_made = sem("consts_made")
        k_ones = sem("k_ones")
        o_zeroed = sem("o_zeroed")
        passed = sem("passed")
        small_in = sem("small_in")
        w_raw = [sem(f"w_raw{k}") for k in range(4)]
        w_hi = sem("w_hi")
        w_lo = sem("w_lo")
        gates_made = sem("gates_made")
        bias_made = sem("bias_made")
        setup = sem("setup")
        trig = sem("trig")
        tables = sem("tables")
        x_in = [sem(f"x_in{t}") for t in range(2)]
        ctx_in = sem("ctx_in")
        ctx_split = sem("ctx_split")
        st_made = sem("st_made")
        mv_made = sem("mv_made")
        ve_made = sem("ve_made")
        rstd_made = sem("rstd_made")
        xn_made = sem("xn_made")
        p_done = sem("p_done")
        p_taken = sem("p_taken")
        p_hi = sem("p_hi")
        roped = sem("roped")
        turned_out = {x: sem(f"turned_out_{x}") for x in "qk"}
        st_in = [sem(f"st_in{h}") for h in range(2)]
        a_done = sem("a_done")
        max_done = sem("max_done")
        m_done = sem("m_done")
        m_taken = sem("m_taken")
        m_hi = sem("m_hi")
        m_in = sem("m_in")
        b_done = sem("b_done")
        exp_done = sem("exp_done")
        av_done = sem("av_done")
        av_taken = sem("av_taken")
        t_done = sem("t_done")
        t_taken = sem("t_taken")
        t_hi = sem("t_hi")
        rd_made = sem("rd_made")
        res_in = [sem(f"res_in{t}") for t in range(2)]
        res_made = sem("res_made")
        x1_made = sem("x1_made")
        x1_out = [sem(f"x1_out{t}") for t in range(2)]
        f_small = sem("f_small")
        gb_made = sem("gb_made")
        gt_hi = sem("gt_hi")
        gt_lo = sem("gt_lo")
        fx_in = sem("fx_in")
        fxn_made = sem("fxn_made")
        x_done = sem("x_done")
        x_taken = sem("x_taken")
        x_hi = sem("x_hi")
        top_made = sem("top_made")
        route_made = sem("route_made")
        u_done = sem("u_done")
        relu_made = sem("relu_made")
        hid_hi = sem("hid_hi")
        sq_made = sem("sq_made")
        hid_lo = sem("hid_lo")
        d_done = sem("d_done")
        e_done = sem("e_done")
        e_taken = sem("e_taken")
        y_made = sem("y_made")
        z_made = sem("z_made")
        fres_in = sem("fres_in")
        fin = sem("fin")
        out_made = sem("out_made")
        out_out = [sem(f"out_out{u}") for u in range(UT)]

        chunks = []
        for c in range(KC):
            chunks.append((wq[c * P:(c + 1) * P, :], wq_s, c))
        for c in range(CC):
            chunks.append((wkv[c * P:(c + 1) * P, 0:D], wk_s, c))
        for c in range(CC):
            chunks.append((wkv[c * P:(c + 1) * P, D:2 * D], wv_s, c))
        for c in range(KC):
            chunks.append((wout[c * P:(c + 1) * P, :], wo_s, c))
        W1 = len(chunks)

        up_d = up.rearrange("(c p) n -> p c n", p=P)
        ffn_chunks = []
        for m in range(MC):
            ffn_chunks += [("up", m), ("dn", m)]
            if m >= 7 and m < 7 + KC:
                ffn_chunks.append(("ex", m - 7))
        chunk_no = {key: W1 + k for k, key in enumerate(ffn_chunks)}

        w_early = ffn_chunks[:5]

        def w_at(m):
            return ffn_chunks[5 + 3 * m:5 + 3 * (m + 1)]

        def ffn_chunk(key):
            kind, m = key
            if kind == "up":
                return up_d[:, :, m * P:(m + 1) * P], [w[:, :, m * P:(m + 1) * P] for w in up_s]
            if kind == "dn":
                return down[m * P:(m + 1) * P, :], [w[:, m, :] for w in dn_s]
            return wexp[m * P:(m + 1) * P, :], [w[:, m, :] for w in ex_s]

        def raw2(k, key):
            r = y_s[:, k % 4, :]
            return r.rearrange("p (c n) -> p c n", c=KC) if key[0] == "up" else r

        def alone(eng):
            eng.sem_inc(passed, 1)

        block = stack.enter_context(nc.Block())

        def phase1(eng, iteration, ahead=0):
            for i in range(-2, 2):
                iteration(i, i)
            with eng.Fori(0, (B - 4) // 2 - ahead) as trip:
                iteration(2 * trip + 2, 0)
                iteration(2 * trip + 3, 1)
            for i in range(B - 2 - 2 * ahead, B + 1):
                iteration(i, i)

        @block.sync
        def _(sp):
            sp.dma_start(g_att[:], g_x.partition_broadcast(P)).then_inc(small_in, INC)
            sp.dma_start(g_ffn[:], g_f.partition_broadcast(P)).then_inc(small_in, INC)
            sp.dma_start(gbout[:], bout.partition_broadcast(P)).then_inc(small_in, INC)
            sp.dma_start(pos_s, posT).then_inc(small_in, INC)
            for k, (src, _, _) in enumerate(chunks):
                if k >= 4:
                    sp.wait_ge(w_lo, k - 3)
                sp.dma_start(raw1[k % 4], src).then_inc(w_raw[k % 4], INC)

            def load_x(b):
                for t in range(TT):
                    n = b * TT + t
                    if some(n - 1):
                        sp.wait_ge(xn_made, n - 1)
                    alone(sp)
                    sp.dma_start(xin[t][:], xt_d[n]).then_inc(x_in[t], INC)
                if some(b):
                    sp.wait_ge(ctx_split, 2 * b)
                alone(sp)
                sp.dma_start(ctx_raw[:], ctx_d[b]).then_inc(ctx_in, INC)

            def store_turned(b, par):
                if some(b - 1):
                    for half in range(2):
                        sp.wait_ge(st_in[half], INC * STACK_DMAS * (b - 1))
                        alone(sp)
                for dst, src, last_job in zip(qk_d[par], (qT, kT), ("qT1", "kT1")):
                    sp.wait_ge(p_taken, len(PREP_JOBS) * b + PREP_JOBS.index(last_job) + 1)
                    alone(sp)
                    for part in range(2):
                        sp.dma_start(dst[part].rearrange("(c p) s -> p c s", p=P),
                                     src[part][:].bitcast(F32)).then_inc(turned_out[last_job[0]], INC)

            def load_stacks(b, par, half):
                if some((b - 2) * STEPS + 8 * (half + 1)):
                    sp.wait_ge(b_done, (b - 2) * STEPS + 8 * (half + 1))
                    alone(sp)
                slots = slice(8 * half, 8 * half + 8)
                for name, dst, src, parts in (("q", st_q[par], qk_d[par][0], Q_PARTS),
                                              ("k", st_k[par], qk_d[par][1], K_PARTS)):
                    sp.wait_ge(turned_out[name], 2 * INC * (b + 1))
                    alone(sp)
                    for r, part in enumerate(parts):
                        heads = src[part].rearrange("(l q d) s -> q d l s", q=2, d=HD)
                        for q in range(2):
                            row = 64 * q + HD * r
                            sp.dma_start(dst[row:row + HD, slots, :].bitcast(F32),
                                         heads[q, :, slots, :]).then_inc(st_in[half], INC)

            def load_max(b, par, half):
                sp.wait_ge(m_taken, len(MID_JOBS) * b + MID_JOBS.index(f"m{half}") + 1)
                for part in range(2):
                    for q in range(2):
                        row = 64 * q + ROWS_A + part
                        sp.dma_start(st_q[par][row:row + 1, 8 * half:8 * half + 8, :].bitcast(F32),
                                     mT[part][q:NH // 2:2, :].bitcast(F32)).then_inc(m_in, INC)

            def iteration(i, par):
                b2, b1, bt = i + 2, i + 1, i - 1

                def store_x1(t):
                    n = bt * TT + t
                    sp.wait_ge(x1_made, n + 1)
                    alone(sp)
                    sp.dma_start(x1_d[n], xres[t][:]).then_inc(x1_out[t], INC)

                if within(b1):
                    load_stacks(b1, (par + 1) % 2, 1)
                if within(i):
                    load_max(i, par % 2, 1)
                if within(bt):
                    for t in range(TT):
                        n = bt * TT + t
                        if some(bt):
                            sp.wait_ge(x1_out[t], INC * bt)
                        alone(sp)
                        sp.dma_start(xres[t][:], xt_d[n]).then_inc(res_in[t], INC)
                    store_x1(0)
                if within(b1):
                    load_max(b1, (par + 1) % 2, 0)
                if within(i + 3):
                    load_x(i + 3)
                if within(b2):
                    store_turned(b2, par % 2)
                    load_stacks(b2, par % 2, 0)
                if within(bt):
                    store_x1(1)

            load_x(0)
            sp.wait_ge(k_ones, 1)
            phase1(sp, iteration, ahead=1)

            for t in range(TT):
                sp.wait_ge(x1_out[t], INC * B)
            sp.dma_start(g_gamma[:], gamma.partition_broadcast(P)).then_inc(f_small, INC)
            sp.dma_start(g_beta[:], beta.partition_broadcast(P)).then_inc(f_small, INC)
            sp.dma_start(gt_raw[:], gate.rearrange("(c p) e -> p c e", p=P)).then_inc(f_small, INC)

            def load_fx(n):
                if some(n):
                    sp.wait_ge(x_done, x_job(n - 1) + 1)
                alone(sp)
                sp.dma_start(fx[:], x1_d[n]).then_inc(fx_in, INC)

            def x_job(n):
                return (UT + 2) * (n // UT) + n % UT

            def load_w(key):
                k = chunk_no[key]
                sp.wait_ge(w_lo, k - 3)
                sp.dma_start(raw2(k, key), ffn_chunk(key)[0]).then_inc(w_raw[k % 4], INC)

            for n in range(UT):
                load_fx(n)
            for key in w_early:
                load_w(key)

            def next_fx(j, u):
                sp.wait_ge(x_done, (UT + 2) * (j + 1) + u if u else (UT + 2) * j + UT)
                alone(sp)
                sp.dma_start(fx[:], x1_d[(j + 1) * UT + u]).then_inc(fx_in, INC)

            def fblock(j, first_block=False, last=False):
                if not first_block:
                    for u in range(UT):
                        n = (j - 1) * UT + u
                        sp.dma_start(fres[:], x1_d[n]).then_inc(fres_in, INC)
                        sp.wait_ge(out_made, n + 1)
                        alone(sp)
                        sp.dma_start(out_d[n], y_s[:, u, :]).then_inc(out_out[u], INC)
                if first_block:
                    for m in range(MC):
                        if m + 2 in X_AT:
                            next_fx(j, X_AT.index(m + 2))
                        for key in w_at(m):
                            load_w(key)
                elif not last:
                    for u in range(UT):
                        next_fx(j, u)

            fblock(0, first_block=True)
            with sp.Fori(0, (NB - 2) // 2) as trip:
                fblock(2 * trip + 1)
                fblock(2 * trip + 2)
            fblock(NB - 1, last=True)
            fblock(NB, last=True)
            for u in range(UT):
                sp.wait_ge(out_out[u], INC * NB)

        @block.gpsimd
        def _(pool):
            nc.gpsimd.memset(ident[:], 0.0).then_inc(ident_made, 1)
            nc.gpsimd.memset(neg_half[:], -0.5)
            for i in range(2):
                last = nc.gpsimd.memset(v_s[i][:, :, :, HD:HD + 1], 1.0)
            last.then_inc(consts_made, 1)
            pool.wait_ge(ident_made, 1)
            nc.gpsimd.affine_select(out=ident[:], in_=ident[:], compare_op=ALU.not_equal, fill=1.0, base=0,
                                    pattern=[[-1, P]], channel_multiplier=1).then_inc(ident_made, 1)

            def inv_std(count):
                pool.wait_ge(mv_made, count)
                if some(count - 1):
                    pool.wait_ge(rstd_made, count - 1)
                alone(pool)
                nc.gpsimd.tensor_scalar_add(var_eps[:], meanvar[:, 1:2], EPS).then_inc(ve_made, 1)
                pool.wait_ge(ve_made, count)
                nc.gpsimd.tensor_tensor(rstd[:], var_eps[:], neg_half[:], ALU.pow).then_inc(rstd_made, 1)

            def rope_sum(b, name):
                r = ROPES.index(name)
                pool.wait_ge(p_taken, len(PREP_JOBS) * b + PREP_JOBS.index(name) + 1)
                t1 = rot[name[0]]
                nc.gpsimd.tensor_tensor(t1[:], t1[:], rot2[:], ALU.add).then_inc(roped, 1)

            def split_ctx(b, par):
                pool.wait_ge(ctx_in, INC * (b + 1))
                hi, lo = ctx_s[par]
                if some(b - 1):
                    pool.wait_ge(m_done, len(MID_JOBS) * (b - 2) + V_DONE)
                alone(pool)
                nc.gpsimd.tensor_copy(hi[:], ctx_raw[:]).then_inc(ctx_split, 1)
                pool.wait_ge(ctx_split, 2 * b + 1)
                nc.gpsimd.tensor_tensor(lo[:], ctx_raw[:], hi[:].bitcast(F32), ALU.subtract).then_inc(ctx_split, 1)

            def iteration(i, par):
                b2, bt = i + 2, i - 1
                if within(b2):
                    for what in POOL_ORDER[:3]:
                        inv_std(b2 * TT + what + 1) if isinstance(what, int) else rope_sum(b2, what)
                if within(bt):
                    if isinstance(i, int) and bt == 0:
                        pool.wait_ge(bias_made, 1)
                    for t in range(TT):
                        pool.wait_ge(res_in[t], INC * (bt + 1))
                        nc.gpsimd.tensor_tensor(xres[t][:], xres[t][:], gbout[:], ALU.add).then_inc(res_made, 1)
                if within(b2):
                    for what in POOL_ORDER[3:]:
                        inv_std(b2 * TT + what + 1) if isinstance(what, int) else rope_sum(b2, what)
                if within(i + 3):
                    split_ctx(i + 3, (par + 1) % 2)

            split_ctx(0, 0)
            phase1(pool, iteration, ahead=1)

            def ffn_inv_std(count):
                inv_std(NT + count)

            def finish_y(j, u, count):
                n = j * UT + u
                ffn_inv_std(count)
                y = y_s[:, u, :]
                pool.wait_ge(z_made, n + 1)
                nc.gpsimd.tensor_tensor(y, y, g_gamma[:], ALU.mult).then_inc(fin, 1)
                pool.wait_ge(fres_in, INC * (n + 1))
                nc.gpsimd.tensor_tensor(fres[:], fres[:], g_beta[:], ALU.add).then_inc(fin, 1)
                pool.wait_ge(fin, 2 * n + 2)
                nc.gpsimd.tensor_tensor(y, y, fres[:], ALU.add).then_inc(out_made, 1)

            for u in range(UT):
                ffn_inv_std(u + 1)
            pool.wait_ge(gb_made, 2)

            def fblock(j, first_block=False, last=False):
                done = 2 * UT * j
                if not first_block:
                    for u in range(UT):
                        finish_y(j - 1, u, done + u + 1)
                if not last:
                    for u in range(UT):
                        ffn_inv_std(done + UT + u + 1)

            fblock(0, first_block=True)
            with pool.Fori(0, (NB - 2) // 2) as trip:
                fblock(2 * trip + 1)
                fblock(2 * trip + 2)
            fblock(NB - 1, last=True)
            for u in range(UT):
                finish_y(NB - 1, u, 2 * UT * NB - UT + u + 1)

        @block.scalar
        def _(act):
            act.wait_ge(setup, 8)
            nc.scalar.activation(sin_a, ang.rearrange("p n a j -> p n (a j)"), ACT.Sin).then_inc(trig, 1)
            nc.scalar.activation(cos_a, turns.rearrange("p n a j -> p n (a j)"), ACT.Sin).then_inc(trig, 1)
            act.wait_ge(small_in, INC * 4)
            nc.scalar.activation(g_att[:], g_att[:], ACT.Tanh).then_inc(gates_made, 1)
            nc.scalar.activation(g_ffn[:], g_ffn[:], ACT.Tanh).then_inc(gates_made, 1)
            for k, (_, dst, c) in enumerate(chunks):
                act.wait_ge(w_raw[k % 4], INC * (k // 4 + 1))
                nc.scalar.copy(dst[0][:, c, :], raw1[k % 4]).then_inc(w_hi, 1)

            def job(kind, name, i, par):
                if kind == "p":
                    b, par = i + 2, par % 2
                    if not within(b) or name not in PREP_SPLITS:
                        return
                    act.wait_ge(p_done, len(PREP_JOBS) * b + PREP_JOBS.index(name) + 1)
                    psum = pP[:, :].rearrange("p (c s) -> p c s", c=KC)
                    t = int(name[-1])
                    if name[0] == "X":
                        nc.scalar.copy(xnT[0][:], psum).then_inc(p_hi, 1)
                        return
                    if some(b):
                        act.wait_ge(turned_out[name[0]], 2 * INC * b)
                    if name[0] == "q":
                        nc.scalar.mul(qT[0][:, :, t * P:(t + 1) * P], psum, SCALE).then_inc(p_hi, 1)
                    else:
                        nc.scalar.copy(kT[0][:, :, t * P:(t + 1) * P], psum).then_inc(p_hi, 1)
                elif kind in "mn":
                    b = i + 1 if kind == "m" else i
                    par = (par + 1) % 2 if kind == "m" else par % 2
                    if not within(b):
                        return
                    act.wait_ge(m_done, len(MID_JOBS) * b + MID_JOBS.index(name) + 1)
                    k = int(name[-1])
                    if name[0] == "V":
                        if some(b - 1):
                            act.wait_ge(av_done, GROUPS * (b - 1))
                        nc.scalar.copy(v_s[par][:, k, :, 0:HD],
                                       pM[:, :].rearrange("p (h e) -> p h e", h=NH)).then_inc(m_taken, 1)
                    else:
                        if some(2 * b + k):
                            act.wait_ge(m_in, 4 * INC * (2 * b + k))
                        nc.scalar.copy(mT[0][:], pM[0:NH // 2, 0:S]).then_inc(m_hi, 1)
                else:
                    b = i - 1 if kind == "t" else i
                    if not within(b) or name[:2] != "aT":
                        return
                    act.wait_ge(t_done, len(TAIL_JOBS) * b + TAIL_JOBS.index(name) + 1)
                    nc.scalar.copy(aT[0][:], pT[:, :].rearrange("p (c s) -> p c s", c=KC)).then_inc(t_hi, 1)

            def take_av(b, g):
                act.wait_ge(av_done, GROUPS * b + g + 1)
                need = len(TAIL_JOBS) * (b - 1) + (2 if g < GROUPS // 2 else 4)
                if some(need):
                    act.wait_ge(t_done, need)
                nc.scalar.copy(av_s[:, g, :], pO[:, 0:S]).then_inc(av_taken, 1)

            def iteration(i, par):
                for s in range(STEPS):
                    for item in SLOTS.get((s, 0), []):
                        if item[-1] != "<":
                            job(item[0], item[2:], i, par)
                    if within(i):
                        if s >= 2 and s % 2 == 0:
                            take_av(i, s // 2 - 1)
                        act.wait_ge(b_done, STEPS * i + s + 1)
                        if some(GROUPS * i + s // 2 - 1):
                            act.wait_ge(av_done, GROUPS * i + s // 2 - 1)
                        nc.scalar.activation(probs[:, s % 4, :, :, :].rearrange("p a b s -> p a (b s)"),
                                             pB[:, :, :], ACT.Exp).then_inc(exp_done, 1)
                    for item in SLOTS.get((s, 1), []):
                        if item[-1] != "<":
                            job(item[0], item[2:], i, par)
                if within(i):
                    take_av(i, GROUPS - 1)

            phase1(act, iteration)

            for t in range(TT):
                act.wait_ge(x1_out[t], INC * B)
            act.wait_ge(f_small, 3 * INC)
            nc.scalar.copy(gt_s[0][:], gt_raw[:]).then_inc(gt_hi, 1)

            def split(key):
                k = chunk_no[key]
                act.wait_ge(w_raw[k % 4], INC * (k // 4 + 1))
                nc.scalar.copy(ffn_chunk(key)[1][0], raw2(k, key)).then_inc(w_hi, 1)

            def turned(j, par, u):
                act.wait_ge(x_done, (UT + 2) * j + u + 1)
                nc.scalar.copy(fT[par][0][:, :, u * P:(u + 1) * P],
                               pX.rearrange("p (c s) -> p c s", c=KC)).then_inc(x_hi, 1)

            def fblock(j, par, first_block=False, last=False):
                for m in range(MC):
                    a = MC * j + m
                    act.wait_ge(u_done, a + 1)
                    if some(a - 1):
                        act.wait_ge(hid_lo, a - 1)
                    nc.scalar.activation(relu[m % 2][:], pU[m % 2], ACT.Relu).then_inc(relu_made, 1)
                    act.wait_ge(relu_made, a + 1)
                    if some(a - 1):
                        act.wait_ge(d_done, a - 1)
                    nc.scalar.activation(hid[m % 2][0][:], relu[m % 2][:], ACT.Square).then_inc(hid_hi, 1)
                    if m == 1:
                        act.wait_ge(x_done, (UT + 2) * j + UT + 1)
                        nc.scalar.copy(gl[:], pX[0:NEXP, :]).then_inc(x_taken, 1)
                    if not last and m in X_AT:
                        turned(j + 1, (par + 1) % 2, X_AT.index(m))
                    if m in E_AT:
                        u = E_AT.index(m)
                        expert_out(j, par, u)
                    if first_block:
                        for key in w_at(m):
                            split(key)

            def expert_out(j, par, u):
                act.wait_ge(e_done, UT * j + u + 1)
                act.wait_ge(route_made, j + 1)
                if isinstance(j, int) and j == 0:
                    act.wait_ge(w_lo, W1 + len(ffn_chunks))
                else:
                    act.wait_ge(out_out[u], INC * j)
                nc.scalar.activation(y_s[:, u, :], pE, ACT.Copy,
                                     scale=route[par % 2][:, u:u + 1]).then_inc(e_taken, 1)

            for u in range(UT):
                turned(0, 0, u)
            for key in w_early:
                split(key)
            fblock(0, 0, first_block=True)
            with act.Fori(0, (NB - 2) // 2) as trip:
                fblock(2 * trip + 1, 1)
                fblock(2 * trip + 2, 0)
            fblock(NB - 1, 1, last=True)

        @block.tensor
        def _(pe):
            pe.wait_ge(ident_made, 2)
            pe.wait_ge(o_zeroed, 1)
            pe.wait_ge(consts_made, 1)
            pe.wait_ge(w_lo, W1)

            def product(dst, lhs, rhs, chunks_, half=None):
                low = chunks_ // 2 if half == 1 else 0
                high = chunks_ // 2 if half == 0 else chunks_
                for c in range(low, high):
                    for a, w in PASSES:
                        last = nc.tensor.matmul(dst, lhs(a, c), rhs(w, c), start=(c == 0 and (a, w) == PASSES[0]),
                                                stop=(c == chunks_ - 1 and (a, w) == PASSES[-1]))
                return last

            def turn(dst, src):
                for c in range(KC):
                    last = nc.tensor.transpose(dst[:, c * P:(c + 1) * P], src(c), ident[:])
                return last

            def job(kind, name, i, par):
                name, half = (name[:-1], 0) if name[-1] == "<" else (name, 1 if name in CUT else None)
                if kind == "p":
                    b, par = i + 2, par % 2
                    if not within(b):
                        return
                    pos = PREP_JOBS.index(name)
                    if half != 1 and some(len(PREP_JOBS) * b + pos):
                        pe.wait_ge(p_taken, len(PREP_JOBS) * b + pos)
                    t = int(name[-1])
                    if name[0] == "X":
                        pe.wait_ge(xn_made, TT * b + t + 1)
                        last = turn(pP, lambda c: xn[:, c * P:(c + 1) * P])
                    elif name[0] == "Q":
                        last = product(pP[:, :], lambda a, c: xnT[a][:, c, :], lambda w, c: wq_s[w][:, c, :], KC,
                                       half)
                    elif name[0] == "K":
                        pe.wait_ge(ctx_split, 2 * b + 2)
                        last = product(pP[:, :], lambda a, c: ctx_s[par][a][:, c, t * P:(t + 1) * P],
                                       lambda w, c: wk_s[w][:, c, :], CC)
                    else:
                        src = rot[name[0].upper()]
                        pe.wait_ge(roped, len(ROPES) * b + ROPES.index(name[0].upper() + name[-1]) + 1)
                        last = turn(pP, lambda c: src[:, c * P:(c + 1) * P])
                    if half != 0:
                        last.then_inc(p_done, 1)
                elif kind in "mn":
                    b = i + 1 if kind == "m" else i
                    par = (par + 1) % 2 if kind == "m" else par % 2
                    if not within(b):
                        return
                    pos = MID_JOBS.index(name)
                    k = int(name[-1])
                    if some(len(MID_JOBS) * b + pos):
                        pe.wait_ge(m_taken, len(MID_JOBS) * b + pos)
                    if name[0] == "V":
                        last = product(pM[:, :], lambda a, c: ctx_s[par][a][:, c, k * P:(k + 1) * P],
                                       lambda w, c: wv_s[w][:, c, :], CC)
                    else:
                        pe.wait_ge(max_done, STEPS * b + 8 * (k + 1))
                        for t in range(TT):
                            last = nc.tensor.transpose(pM[0:NH // 2, t * P:(t + 1) * P],
                                                       mneg[par][:, t, k * 16:(k + 1) * 16], ident[:])
                    last.then_inc(m_done, 1)
                else:
                    b = i - 1 if kind == "t" else i
                    if not within(b):
                        return
                    pos = TAIL_JOBS.index(name)
                    if half != 1 and some(len(TAIL_JOBS) * b + pos):
                        pe.wait_ge(t_taken, len(TAIL_JOBS) * b + pos)
                    if name[:2] == "aT":
                        last = turn(pT, lambda c: attn[int(name[-1])][:, c * P:(c + 1) * P])
                    elif name[0] == "O":
                        last = product(pT[:, :], lambda a, c: aT[a][:, c, :], lambda w, c: wo_s[w][:, c, :], KC,
                                       half)
                    else:
                        t, heads = int(name[1]), int(name[2])
                        pe.wait_ge(av_taken, GROUPS * b + GROUPS // 2 * (heads + 1))
                        last = turn(pT, lambda c: av_s[:, GROUPS // 2 * heads + c, t * P:(t + 1) * P])
                    if half != 0:
                        last.then_inc(t_done, 1)

            def logits_a(b, par, s):
                if s % 8 == 0:
                    pe.wait_ge(st_in[s // 8], INC * STACK_DMAS * (b + 1))
                if some(STEPS * b + s):
                    pe.wait_ge(max_done, STEPS * b + s)
                for t in range(TT):
                    for q in range(2):
                        rows = slice(64 * q, 64 * q + ROWS_A)
                        last = nc.tensor.matmul(pA[:, q, t * S:(t + 1) * S], st_q[par][rows, s, t * P:(t + 1) * P],
                                                st_k[par][rows, s, :], start=True, stop=True)
                last.then_inc(a_done, 1)

            def logits_b(b, par, s):
                if s % 8 == 0:
                    pe.wait_ge(m_in, 4 * INC * (2 * b + s // 8 + 1))
                if some(STEPS * b + s):
                    pe.wait_ge(exp_done, STEPS * b + s)
                for t in range(TT):
                    for q in range(2):
                        rows = slice(64 * q, 64 * q + ROWS_B)
                        last = nc.tensor.matmul(pB[:, q, t * S:(t + 1) * S], st_k[par][rows, s, t * P:(t + 1) * P],
                                                st_q[par][rows, s, :], start=True, stop=True)
                last.then_inc(b_done, 1)

            def times_v(b, par, g):
                pe.wait_ge(exp_done, STEPS * b + 2 * g + 2)
                if g == 0:
                    pe.wait_ge(m_taken, len(MID_JOBS) * b + V_DONE)
                if some(GROUPS * b + g):
                    pe.wait_ge(av_taken, GROUPS * b + g)
                for t in range(TT):
                    for j in range(4):
                        last = nc.tensor.matmul(pO[32 * j:32 * j + HD + 1, 0:S], v_s[par][:, t, 4 * g + j, :],
                                                probs[:, (2 * g + j // 2) % 4, j % 2, t, :],
                                                start=(t == 0), stop=(t == TT - 1))
                last.then_inc(av_done, 1)

            def iteration(i, par):
                for s in range(STEPS):
                    if within(i + 1):
                        logits_a(i + 1, (par + 1) % 2, s)
                    for item in SLOTS.get((s, 0), []):
                        job(item[0], item[2:], i, par)
                    if within(i):
                        if s >= 2 and s % 2 == 0:
                            times_v(i, par % 2, s // 2 - 1)
                        logits_b(i, par % 2, s)
                    for item in SLOTS.get((s, 1), []):
                        job(item[0], item[2:], i, par)
                if within(i):
                    times_v(i, par % 2, GROUPS - 1)

            phase1(pe, iteration)

            def turned(j, u):
                n = UT * j + u
                pe.wait_ge(fxn_made, n + 1)
                if some((UT + 2) * j + u):
                    pe.wait_ge(x_taken, (UT + 2) * j + u)
                turn(pX, lambda c: fx[:, c * P:(c + 1) * P]).then_inc(x_done, 1)

            def routing(j, par):
                pe.wait_ge(x_taken, (UT + 2) * j + UT)
                product(pX[0:NEXP, :], lambda a, c: gt_s[a][:, c, :], lambda w, c: fT[par][w][:, c, :],
                        KC).then_inc(x_done, 1)

            def routing_turned(j):
                pe.wait_ge(x_taken, (UT + 2) * j + UT + 1)
                alone(pe)
                for u in range(UT):
                    last = nc.tensor.transpose(pX[:, u * NEXP:(u + 1) * NEXP], gl[:, u * P:(u + 1) * P],
                                               ident[0:NEXP, 0:NEXP])
                last.then_inc(x_done, 1)

            def hidden(j, par, m, first_block):
                a = MC * j + m
                if some(a - 1):
                    pe.wait_ge(relu_made, a - 1)
                if m == 0:
                    pe.wait_ge(x_taken, (UT + 2) * j + UT)
                if first_block:
                    pe.wait_ge(w_lo, chunk_no["up", m] + 1)
                product(pU[m % 2], lambda x_, c: up_s[x_][:, c, m * P:(m + 1) * P],
                        lambda w, c: fT[par][w][:, c, :], KC).then_inc(u_done, 1)

            def shared(j, m, first_block):
                a = MC * j + m
                pe.wait_ge(hid_lo, a + 1)
                if m == 0 and some(UT * j):
                    pe.wait_ge(y_made, UT * j)
                if first_block:
                    pe.wait_ge(w_lo, chunk_no["dn", m] + 1)
                for u in range(UT):
                    for k, (x_, w) in enumerate(PASSES):
                        last = nc.tensor.matmul(acc[u], hid[m % 2][x_][:, u * P:(u + 1) * P], dn_s[w][:, m, :],
                                                start=(m == 0 and k == 0), stop=(m == MC - 1 and k == 2))
                last.then_inc(d_done, 1)

            def expert(j, par, u, first_block):
                if first_block:
                    pe.wait_ge(w_lo, chunk_no["ex", KC - 1] + 1)
                if some(UT * j + u):
                    pe.wait_ge(e_taken, UT * j + u)
                product(pE, lambda a, c: fT[par][a][:, c, u * P:(u + 1) * P], lambda w, c: ex_s[w][:, c, :],
                        KC).then_inc(e_done, 1)

            def fblock(j, par, first_block=False, last=False):
                for m in range(MC):
                    hidden(j, par, m, first_block)
                    if m == 0:
                        routing(j, par)
                    if m == 2:
                        routing_turned(j)
                    if m >= 1:
                        shared(j, m - 1, first_block)
                    if not last and m in X_AT:
                        turned(j + 1, X_AT.index(m))
                    if m in E_AT:
                        expert(j, par, E_AT.index(m), first_block)
                shared(j, MC - 1, first_block)

            for u in range(UT):
                turned(0, u)
            pe.wait_ge(gt_lo, 1)
            fblock(0, 0, first_block=True)
            with pe.Fori(0, (NB - 2) // 2) as trip:
                fblock(2 * trip + 1, 1)
                fblock(2 * trip + 2, 0)
            fblock(NB - 1, 1, last=True)

        @block.vector
        def _(dve):
            nc.vector.memset(pO[:, :], 0.0).then_inc(o_zeroed, 1)
            for i in range(2):
                for r in (32, 96):
                    last = nc.vector.memset(st_k[i][r:r + 32, :, :].bitcast(F32), 1.0)
            last.then_inc(k_ones, 1)
            dve.wait_ge(small_in, INC * 4)
            for j in range(HALF):
                freq = float(np.float32(ROPE_BASE ** (-j / HALF)))
                last = nc.vector.tensor_scalar(ang[:, :, :, j], pos_s, freq, None, ALU.mult)
            last.then_inc(setup, 1)
            two_pi = 2.0 * float(np.pi)
            hi_pi = float(np.float32(two_pi))
            round_to = 1.5 * 2.0 ** 23
            dve.wait_ge(setup, 1)
            nc.vector.tensor_scalar(turns, ang, 1.0 / two_pi, round_to, ALU.mult, ALU.add).then_inc(setup, 1)
            dve.wait_ge(setup, 2)
            nc.vector.tensor_scalar(turns, turns, -round_to, None, ALU.add).then_inc(setup, 1)
            for k, part in enumerate((hi_pi, two_pi - hi_pi)):
                dve.wait_ge(setup, 3 + k)
                nc.vector.scalar_tensor_tensor(ang, turns, -part, ang, ALU.mult, ALU.add).then_inc(setup, 1)
            dve.wait_ge(setup, 5)
            pi = float(np.float32(3.1415925))
            nc.vector.tensor_scalar(ang, ang, pi, -pi, ALU.min, ALU.max).then_inc(setup, 1)
            dve.wait_ge(setup, 6)
            nc.vector.scalar_tensor_tensor(turns, ang, -1.0, ang, ALU.mult, ALU.min).then_inc(setup, 1)
            dve.wait_ge(setup, 7)
            nc.vector.tensor_scalar(turns, turns, float(np.pi) / 2, None, ALU.add).then_inc(setup, 1)
            dve.wait_ge(trig, 2)
            nc.vector.tensor_copy(cos_t[:, :, :, 0], cos_a)
            nc.vector.tensor_copy(cos_t[:, :, :, 1], cos_a)
            nc.vector.tensor_copy(sin_t[:, :, :, 1], sin_a)
            nc.vector.tensor_scalar(sin_t[:, :, :, 0], sin_a, -1.0, None, ALU.mult).then_inc(tables, 1)
            dve.wait_ge(gates_made, 2)
            nc.vector.tensor_scalar(gbout[:], gbout[:], g_att[:, 0:1], None, ALU.mult).then_inc(bias_made, 1)
            for k, (_, dst, c) in enumerate(chunks):
                dve.wait_ge(w_hi, k + 1)
                nc.vector.tensor_tensor(dst[1][:, c, :], raw1[k % 4], dst[0][:, c, :].bitcast(F32),
                                        ALU.subtract).then_inc(w_lo, 1)
            dve.wait_ge(tables, 1)

            def mean_var(src, count):
                if some(count - 1):
                    dve.wait_ge(mv_made, count - 1)
                nc.vector.bn_stats(stats[:], src).then_inc(st_made, 1)
                dve.wait_ge(st_made, count)
                if some(count - 1):
                    dve.wait_ge(rstd_made, count - 1)
                alone(dve)
                nc.vector.bn_aggr(meanvar[:], stats[:]).then_inc(mv_made, 1)

            def normalise(dst, src, count):
                dve.wait_ge(rstd_made, count)
                return nc.vector.tensor_scalar(dst, src, meanvar[:, 0:1], rstd[:, 0:1], ALU.subtract, ALU.mult)

            def job(kind, name, i, par):
                if kind == "p":
                    b = i + 2
                    if not within(b):
                        return
                    pos = PREP_JOBS.index(name)
                    t = int(name[-1])
                    if name in PREP_SPLITS:
                        dve.wait_ge(p_hi, len(PREP_SPLITS) * b + PREP_SPLITS.index(name) + 1)
                        psum = pP[:, :].rearrange("p (c s) -> p c s", c=KC)
                        if name[0] == "X":
                            op = nc.vector.tensor_tensor(xnT[1][:], psum, xnT[0][:].bitcast(F32), ALU.subtract)
                        else:
                            src, scale = (qT, SCALE) if name[0] == "q" else (kT, 1.0)
                            cut = slice(t * P, (t + 1) * P)
                            op = nc.vector.scalar_tensor_tensor(src[1][:, :, cut], psum, scale,
                                                                src[0][:, :, cut].bitcast(F32),
                                                                ALU.mult, ALU.subtract)
                        op.then_inc(p_taken, 1)
                        return
                    dve.wait_ge(p_done, len(PREP_JOBS) * b + pos + 1)
                    n = TT * b + t
                    xv = pP[:, :].rearrange("p (h k two) -> p h k two", h=NH, two=2)
                    r = ROPES.index(name)

                    def table(a):
                        return a[:, bass.ds(n, 1), :, :].to_broadcast([P, NH, ANG, 2])

                    def view(a):
                        return a[:].rearrange("p (h k two) -> p h k two", h=NH, two=2)

                    nc.vector.tensor_tensor(view(rot[name[0]]), xv, table(cos_t), ALU.mult)
                    if some(len(ROPES) * b + r):
                        dve.wait_ge(roped, len(ROPES) * b + r)
                    nc.vector.tensor_tensor(view(rot2), xv[:, :, :, ::-1], table(sin_t), ALU.mult).then_inc(p_taken, 1)
                elif kind in "mn":
                    b = i + 1 if kind == "m" else i
                    if not within(b) or name[0] == "V":
                        return
                    dve.wait_ge(m_hi, 2 * b + int(name[-1]) + 1)
                    nc.vector.tensor_tensor(mT[1][:], pM[0:NH // 2, 0:S], mT[0][:].bitcast(F32),
                                            ALU.subtract).then_inc(m_taken, 1)
                else:
                    b = i - 1 if kind == "t" else i
                    if not within(b):
                        return
                    pos = TAIL_JOBS.index(name)
                    t = int(name[-1]) if name[0] != "a" or name[1] == "T" else int(name[1])
                    if name[:2] == "aT":
                        dve.wait_ge(t_hi, TT * b + t + 1)
                        nc.vector.tensor_tensor(aT[1][:], pT[:, :].rearrange("p (c s) -> p c s", c=KC),
                                                aT[0][:].bitcast(F32), ALU.subtract).then_inc(t_taken, 1)
                        return
                    dve.wait_ge(t_done, len(TAIL_JOBS) * b + pos + 1)
                    if name[0] == "O":
                        n = TT * b + t
                        dve.wait_ge(res_made, n + 1)
                        nc.vector.scalar_tensor_tensor(xres[t][:], pT[:, :], g_att[:, 0:1], xres[t][:],
                                                       ALU.mult, ALU.add).then_inc(x1_made, 1)
                        dve.wait_ge(x1_made, n + 1)
                        nc.vector.nop().then_inc(t_taken, 1)
                        return
                    half = int(name[2])
                    heads = pT[:, :].rearrange("p (h e) -> p h e", e=32)
                    c = 4 * b + pos
                    nc.vector.reciprocal(rden[:], heads[:, :, HD]).then_inc(rd_made, 1)
                    dve.wait_ge(rd_made, c + 1)
                    nc.vector.tensor_tensor(
                        attn[t][:, half * D // 2:(half + 1) * D // 2].rearrange("p (h e) -> p h e", e=HD),
                        heads[:, :, 0:HD], rden[:].unsqueeze(2).to_broadcast([P, NH // 2, HD]),
                        ALU.mult).then_inc(t_taken, 1)

            def iteration(i, par):
                for s in range(STEPS):
                    if within(i + 2):
                        for t, at in enumerate(LN_AT):
                            n = TT * (i + 2) + t
                            if s == at:
                                dve.wait_ge(x_in[t], INC * (i + 3))
                                mean_var(xin[t][:], n + 1)
                            if s == at + 1:
                                if some(n):
                                    before = len(PREP_JOBS) * (i + 1 + t) + PREP_JOBS.index(f"X{1 - t}") + 1
                                    dve.wait_ge(p_done, before)
                                normalise(xn[:], xin[t][:], n + 1).then_inc(xn_made, 1)
                    if within(i + 1):
                        b = i + 1
                        dve.wait_ge(a_done, STEPS * b + s + 1)
                        nc.vector.tensor_reduce(
                            mneg[(par + 1) % 2][:, :, 2 * s:2 * s + 2].rearrange("p t q -> p q t"),
                            pA[:, :, :].rearrange("p q (t k) -> p q t k", t=TT), AX.X, ALU.max,
                            negate=True).then_inc(max_done, 1)
                    for slot in range(2):
                        for item in SLOTS.get((s, slot), []):
                            if item[-1] != "<":
                                job(item[0], item[2:], i, par)

            phase1(dve, iteration)

            for t in range(TT):
                dve.wait_ge(x1_out[t], INC * B)
            dve.wait_ge(f_small, 3 * INC)
            nc.vector.tensor_scalar(g_gamma[:], g_gamma[:], g_ffn[:, 0:1], None, ALU.mult).then_inc(gb_made, 1)
            nc.vector.tensor_scalar(g_beta[:], g_beta[:], g_ffn[:, 0:1], None, ALU.mult).then_inc(gb_made, 1)
            dve.wait_ge(gt_hi, 1)
            nc.vector.tensor_tensor(gt_s[1][:], gt_raw[:], gt_s[0][:].bitcast(F32), ALU.subtract).then_inc(gt_lo, 1)

            def split(key):
                k = chunk_no[key]
                dve.wait_ge(w_hi, k + 1)
                hi, lo = ffn_chunk(key)[1]
                nc.vector.tensor_tensor(lo, raw2(k, key), hi.bitcast(F32), ALU.subtract).then_inc(w_lo, 1)

            def norm_in(n, count):
                dve.wait_ge(fx_in, INC * (n + 1))
                mean_var(fx[:], NT + count)
                normalise(fx[:], fx[:], NT + count).then_inc(fxn_made, 1)

            def turned(j, par, u):
                dve.wait_ge(x_hi, UT * j + u + 1)
                cut = slice(u * P, (u + 1) * P)
                nc.vector.tensor_tensor(fT[par][1][:, :, cut], pX.rearrange("p (c s) -> p c s", c=KC),
                                        fT[par][0][:, :, cut].bitcast(F32), ALU.subtract).then_inc(x_taken, 1)

            def sum_y(j):
                for u in range(UT):
                    if u == 0:
                        dve.wait_ge(d_done, MC * (j + 1))
                    dve.wait_ge(e_taken, UT * j + u + 1)
                    nc.vector.tensor_tensor(y_s[:, u, :], acc[u], y_s[:, u, :], ALU.add).then_inc(y_made, 1)

            def norm_y(j, u, count):
                n = UT * j + u
                dve.wait_ge(y_made, n + 1)
                mean_var(y_s[:, u, :], NT + count)
                normalise(y_s[:, u, :], y_s[:, u, :], NT + count).then_inc(z_made, 1)

            def fblock(j, par, first_block=False, last=False):
                done = 2 * UT * j
                if not first_block:
                    sum_y(j - 1)
                for m in range(MC):
                    a = MC * j + m
                    r = relu[m % 2]
                    dve.wait_ge(hid_hi, a + 1)
                    nc.vector.tensor_tensor(r[:], r[:], r[:], ALU.mult).then_inc(sq_made, 1)
                    dve.wait_ge(sq_made, a + 1)
                    nc.vector.tensor_tensor(hid[m % 2][1][:], r[:], hid[m % 2][0][:].bitcast(F32),
                                            ALU.subtract).then_inc(hid_lo, 1)
                    if m == 3:
                        dve.wait_ge(x_done, (UT + 2) * j + UT + 2)
                        nc.vector.tensor_copy(glT[:], pX[:, 0:UT * NEXP].rearrange("p (u e) -> p u e", u=UT)
                                              ).then_inc(x_taken, 1)
                        dve.wait_ge(x_taken, (UT + 2) * j + UT + 2)
                        alone(dve)
                        for u in range(UT):
                            last_op = nc.vector.max(top[:, u, :], glT[:, u, :])
                        last_op.then_inc(top_made, 1)
                        dve.wait_ge(top_made, j + 1)
                        nc.vector.tensor_tensor(route[par % 2][:], top[:, :, 0], top[:, :, 1],
                                                ALU.add).then_inc(route_made, 1)
                    if not first_block and m < UT:
                        norm_y(j - 1, m, done + m + 1)
                    if not last and m + 1 in X_AT:
                        u = X_AT.index(m + 1)
                        norm_in(UT * (j + 1) + u, done + UT + u + 1)
                    if not last and m in X_AT:
                        turned(j + 1, (par + 1) % 2, X_AT.index(m))
                    if first_block:
                        for key in w_at(m):
                            split(key)

            for u in range(UT):
                norm_in(u, u + 1)
                turned(0, 0, u)
            for key in w_early:
                split(key)
            fblock(0, 0, first_block=True)
            with dve.Fori(0, (NB - 2) // 2) as trip:
                fblock(2 * trip + 1, 1)
                fblock(2 * trip + 2, 0)
            fblock(NB - 1, 1, last=True)
            sum_y(NB - 1)
            for u in range(UT):
                norm_y(NB - 1, u, 2 * UT * NB - UT + u + 1)


X_AT = (5, 7, 9, 11)
E_AT = (12, 13, 14, 15)


def kernel(**inputs):
    import concourse.bacc as bacc
    from concourse.bass_utils import run_bass_kernel_spmd

    a = {k: np.asarray(v) for k, v in inputs.items()}
    pos = a["fside_BxSx2_0"].reshape(NT, P, POS)
    arrays = {
        "x": a["x"],
        "ctxT": a["ctx_1024"].transpose(0, 2, 1),
        "posT": pos.transpose(1, 0, 2),
        "g_x": a["g_xattn"],
        "g_f": a["g_ffn"],
        "wq": a["L0_xattn_Wq"],
        "wkv": a["L0_xattn_Wkv"],
        "wout": a["L0_xattn_Wout"],
        "bout": a["L0_xattn_bout"],
        "gate": a["L0_ffn_gate_w"],
        "up": a["L0_ffn_up_w"],
        "down": a["L0_ffn_down_w"],
        "wexp": a["L0_ffn_expert_weight"],
        "gamma": a["L0_ffn_ln_gamma"],
        "beta": a["L0_ffn_ln_beta"],
    }
    arrays = {k: np.ascontiguousarray(v) for k, v in arrays.items()}
    nc = bacc.Bacc("TRN2", target_bir_lowering=False, num_devices=1)
    args = [nc.dram_tensor(k, v.shape, mybir.dt.from_np(v.dtype), kind="ExternalInput").ap()
            for k, v in arrays.items()]
    out = nc.dram_tensor("out", (B, S, D), F32, kind="ExternalOutput").ap()
    flamingo_gated(nc, *args, out)
    r = run_bass_kernel_spmd(nc, [arrays], core_ids=[0])
    return r.results[0]["out"]
```

```python
from contextlib import ExitStack

import numpy as np

import concourse.bass as bass
from concourse import mybir
from concourse.alu_op_type import AluOpType as ALU

F32 = mybir.dt.float32
F32R = mybir.dt.float32r
ACT = mybir.ActivationFunctionType
AX = mybir.AxisListType

P = 128
B, S, D = 16, 256, 512
CD = 256
NH, HD = 32, 16
INTER, NEXP = 2048, 8
EPS = 1e-5
ROPE_BASE = 10000.0
POS = 2
HALF = HD // POS // 2
ANG = POS * HALF
TT = S // P
KC = D // P
CC = CD // P
NT = B * TT
STEPS = NH // 2
GROUPS = NH // 4
SCALE = 1.0 / float(np.sqrt(HD))
MC = INTER // P
BLK = 512
NB = B * S // BLK
UT = BLK // P
INC = 16

Q_PARTS = (0, 1, 0)
K_PARTS = (0, 0, 1)
ROWS_A = 3 * HD
ROWS_B = ROWS_A + 2
STACK_DMAS = 2 * len(Q_PARTS) * 2
PASSES = ((0, 0), (1, 0), (0, 1))

PREP_JOBS = ("K0", "X0", "Q0", "kT0", "qT0", "X1", "Q1", "K1", "qT1", "kT1")
PREP_SPLITS = tuple(job for job in PREP_JOBS if job[0] == "X" or job[1] == "T")
ROPES = tuple(job for job in PREP_JOBS if job[0] in "QK")
MID_JOBS = ("m0", "V0", "V1", "m1")
V_DONE = MID_JOBS.index("V1") + 1
POOL_ORDER = (0, "K0", "Q0", 1, "Q1", "K1")
TAIL_JOBS = ("a00", "a10", "a01", "a11", "aT0", "O0", "aT1", "O1")
LATE = 3
LN_AT = (0, 5)

SLOTS = {
    (0, 1): ["p:K0"],
    (1, 1): ["n:m1", "p:X0", "t:a01"],
    (2, 1): ["p:Q0<"],
    (3, 0): ["p:Q0"],
    (3, 1): ["t:a11"],
    (4, 1): ["p:kT0", "t:aT0"],
    (5, 0): ["p:qT0"],
    (5, 1): ["t:O0<"],
    (6, 1): ["t:O0", "p:X1"],
    (7, 1): ["t:aT1", "p:Q1<"],
    (8, 0): ["p:Q1"],
    (9, 0): ["m:m0"],
    (9, 1): ["p:K1"],
    (10, 0): ["t:O1<", "p:qT1"],
    (11, 0): ["p:kT1", "t:O1"],
    (13, 0): ["m:V0", "h:a00"],
    (14, 0): ["h:a10"],
    (14, 1): ["m:V1"],
}


X_AT = (6, 8, 10, 12)
E_AT = (12, 13, 14, 15)


def jobs_of(kinds):
    return [(x[0], x[2:]) for at in sorted(SLOTS) for x in SLOTS[at] if x[0] in kinds and x[-1] != "<"]


assert [x for _, x in jobs_of("p")] == list(PREP_JOBS)
assert jobs_of("th") == [("t", x) for x in TAIL_JOBS[2:]] + [("h", x) for x in TAIL_JOBS[:2]]
assert jobs_of("mn") == [("n", MID_JOBS[-1])] + [("m", x) for x in MID_JOBS[:-1]]

CUT = [x[2:-1] for items in SLOTS.values() for x in items if x[-1] == "<"]


def maxima_steps(i, s):
    if isinstance(i, int) and i == -1:
        before = [max(0, min(STEPS, (8 * (n - LATE) + 4) // 5)) for n in (s, s + 1)]
        return list(range(*before))
    return [s]


def some(count):
    return not isinstance(count, int) or count > 0


def within(b):
    return not isinstance(b, int) or 0 <= b < B


def flamingo_gated(nc, x, ctxT, posT, g_x, g_f, wq, wkv, wout, bout, gate, up, down, wexp, gamma, beta, out):
    xt_d = x.rearrange("b (t p) d -> (b t) p d", p=P)
    out_d = out.rearrange("b (t p) d -> (b t) p d", p=P)
    ctx_d = ctxT.rearrange("b (c p) s -> b p c s", p=P)
    qk_d = [[nc.dram_tensor(f"{x}T_scratch{par}", [2, D, S], F32, kind="Internal").ap() for x in "qk"]
            for par in range(2)]
    x1_d = nc.dram_tensor("x1_scratch", [NT, P, D], F32, kind="Internal").ap()

    with ExitStack() as stack:
        def sem(name):
            return stack.enter_context(nc.semaphore(name))

        def bank(name, shape):
            return stack.enter_context(nc.psum_tensor(name, shape, F32))

        pA = bank("pA", [P, 2, 512])
        pB = bank("pB", [P, 2, 512])
        pO = bank("pO", [P, 512])
        pP = bank("pP", [P, 512])
        pM = bank("pM", [P, 512])
        pT = bank("pT", [P, 512])
        acc = [pA[:, 0, :], pA[:, 1, :], pB[:, 0, :], pB[:, 1, :]]
        pU = [pO[:, :], pP[:, :]]
        pE = pT[:, :]
        pX = pM[:, :]

        def keep(name, shape, dt=F32):
            return stack.enter_context(nc.sbuf_tensor(name, shape, dt))

        ident = keep("ident", [P, P])
        g_att = keep("g_att", [P, 1])
        g_ffn = keep("g_ffn", [P, 1])
        neg_half = keep("neg_half", [P, 1])
        stats = keep("stats", [P, 6])
        meanvar = keep("meanvar", [P, 2])
        var_eps = keep("var_eps", [P, 1])
        rstd = keep("rstd", [P, 1])

        first = ExitStack()

        def sb1(name, shape, dt=F32):
            return first.enter_context(nc.sbuf_tensor(name, shape, dt))

        wq_s = [sb1(f"wq{i}", [P, KC, D], F32R) for i in range(2)]
        wk_s = [sb1(f"wk{i}", [P, CC, D], F32R) for i in range(2)]
        wv_s = [sb1(f"wv{i}", [P, CC, D], F32R) for i in range(2)]
        st_q, st_k = [None, None], [None, None]
        st_q[0] = sb1("stq0", [P, STEPS, S], F32R)
        st_k[0] = sb1("stk0", [P, STEPS, S], F32R)
        qT = [sb1(f"qT{i}", [P, KC, S], F32R) for i in range(2)]
        kT = [sb1(f"kT{i}", [P, KC, S], F32R) for i in range(2)]
        ctx_raw = sb1("ctx_raw", [P, CC, S])
        ctx_s = [[sb1(f"ctx{i}{j}", [P, CC, S], F32R) for j in range(2)] for i in range(2)]
        xin = [sb1(f"xin{i}", [P, D]) for i in range(2)]
        xn = sb1("xn", [P, D])
        xnT = [sb1(f"xnT{i}", [P, KC, P], F32R) for i in range(2)]
        rot = {"Q": sb1("rot_q", [P, D]), "K": sb1("rot_k", [P, D])}
        rot2 = sb1("rot2", [P, D])
        cos_t = sb1("cos_t", [P, NT, ANG, 2])
        sin_t = sb1("sin_t", [P, NT, ANG, 2])
        st_q[1] = sb1("stq1", [P, STEPS, S], F32R)
        st_k[1] = sb1("stk1", [P, STEPS, S], F32R)
        probs = sb1("probs", [P, 4, 2, TT, S])
        v_s = [sb1(f"v{i}", [P, TT, NH, HD + 1]) for i in range(2)]
        wo_s = [sb1(f"wo{i}", [P, KC, D], F32R) for i in range(2)]
        av_s = sb1("av_s", [P, GROUPS, S])
        attn = [sb1(f"attn{t}", [P, D]) for t in range(TT)]
        rden = sb1("rden", [P, NH // 2])
        aT = [sb1(f"aT{i}", [P, KC, P], F32R) for i in range(2)]
        xres = [sb1(f"xres{i}", [P, D]) for i in range(2)]
        gbout = sb1("gbout", [P, D])
        mneg = [sb1(f"mneg{i}", [P, TT, NH]) for i in range(2)]
        mT = [sb1(f"mT{i}", [NH // 2, S], F32R) for i in range(2)]

        raw1 = [probs[:, k // 2, k % 2, :, :].rearrange("p t s -> p (t s)") for k in range(8)]
        raw1 += [attn[0][:], attn[1][:], xres[0][:], xres[1][:]]
        pos_s = av_s[:, 0, 0:NT * POS].rearrange("p (n a) -> p n a", a=POS)
        ang = av_s[:, 1, 0:NT * ANG].rearrange("p (n a j) -> p n a j", a=POS, j=HALF)
        turns = av_s[:, 2, 0:NT * ANG].rearrange("p (n a j) -> p n a j", a=POS, j=HALF)
        sin_a = av_s[:, 3, 0:NT * ANG].rearrange("p (n k) -> p n k", k=ANG)
        cos_a = av_s[:, 4, 0:NT * ANG].rearrange("p (n k) -> p n k", k=ANG)
        first.close()

        second = ExitStack()

        def sb2(name, shape, dt=F32):
            return second.enter_context(nc.sbuf_tensor(name, shape, dt))

        up_s = [sb2(f"up{i}", [P, KC, INTER], F32R) for i in range(2)]
        fT = [None, None]
        fT[0] = [sb2(f"fT0{j}", [P, KC, BLK], F32R) for j in range(2)]
        gt_s = [sb2(f"gt{i}", [P, KC, NEXP], F32R) for i in range(2)]
        gt_raw = sb2("gt_raw", [P, KC, NEXP])
        fx = sb2("fx", [P, D])
        gl = fx[0:NEXP, :]
        fres = [sb2(f"fres{k}", [P, D]) for k in range(2)]
        y_s = sb2("y_s", [P, UT, D])
        g_gamma = sb2("g_gamma", [P, D])
        g_beta = sb2("g_beta", [P, D])
        relu = [sb2(f"relu{i}", [P, BLK]) for i in range(2)]
        hid = [[sb2(f"hid{i}{j}", [P, BLK], F32R) for j in range(2)] for i in range(2)]
        dn_s = [sb2(f"dn{i}", [P, MC, D], F32R) for i in range(2)]
        ex_s = [sb2(f"ex{i}", [P, KC, D], F32R) for i in range(2)]
        fT[1] = [sb2(f"fT1{j}", [P, KC, BLK], F32R) for j in range(2)]
        glT = sb2("glT", [P, UT, NEXP])
        top = sb2("top", [P, UT, 8])
        route = [sb2(f"route{i}", [P, UT]) for i in range(2)]
        second.close()

        W1 = 2 * KC + 2 * CC

        ident_made = sem("ident_made")
        consts_made = sem("consts_made")
        k_ones = sem("k_ones")
        o_zeroed = sem("o_zeroed")
        passed = sem("passed")
        small_in = sem("small_in")
        pos_in = sem("pos_in")
        w_raw = [sem(f"w_raw{k}") for k in range(W1)]
        f_raw = [sem(f"f_raw{k}") for k in range(4)]
        w_hi = sem("w_hi")
        w_lo = sem("w_lo")
        gates_made = sem("gates_made")
        bias_made = sem("bias_made")
        setup = sem("setup")
        trig = sem("trig")
        tables = sem("tables")
        x_in = [sem(f"x_in{t}") for t in range(2)]
        ctx_in = sem("ctx_in")
        ctx_split = sem("ctx_split")
        st_made = sem("st_made")
        mv_made = sem("mv_made")
        ve_made = sem("ve_made")
        rstd_made = sem("rstd_made")
        xn_made = sem("xn_made")
        p_done = sem("p_done")
        p_taken = sem("p_taken")
        p_hi = sem("p_hi")
        roped = sem("roped")
        turned_out = {x: sem(f"turned_out_{x}") for x in "qk"}
        st_in = [sem(f"st_in{h}") for h in range(2)]
        a_done = sem("a_done")
        max_done = sem("max_done")
        m_done = sem("m_done")
        m_taken = sem("m_taken")
        m_hi = sem("m_hi")
        m_in = sem("m_in")
        b_done = sem("b_done")
        exp_done = sem("exp_done")
        av_done = sem("av_done")
        av_taken = sem("av_taken")
        t_done = sem("t_done")
        t_taken = sem("t_taken")
        t_hi = sem("t_hi")
        rd_made = sem("rd_made")
        res_in = [sem(f"res_in{t}") for t in range(2)]
        res_made = sem("res_made")
        x1_made = sem("x1_made")
        x1_out = [sem(f"x1_out{t}") for t in range(2)]
        f_small = sem("f_small")
        gb_made = sem("gb_made")
        gt_hi = sem("gt_hi")
        gt_lo = sem("gt_lo")
        fx_in = sem("fx_in")
        fxn_made = sem("fxn_made")
        x_done = sem("x_done")
        x_taken = sem("x_taken")
        x_hi = sem("x_hi")
        top_made = sem("top_made")
        route_made = sem("route_made")
        u_done = sem("u_done")
        relu_made = sem("relu_made")
        hid_hi = sem("hid_hi")
        sq_made = sem("sq_made")
        hid_lo = sem("hid_lo")
        d_done = sem("d_done")
        tile_done = sem("tile_done")
        e_done = sem("e_done")
        e_taken = sem("e_taken")
        y_made = sem("y_made")
        z_made = sem("z_made")
        fres_in = [sem(f"fres_in{k}") for k in range(2)]
        fres_made = sem("fres_made")
        out_made = sem("out_made")
        out_out = [sem(f"out_out{u}") for u in range(UT)]

        chunks = []
        for c in range(CC):
            chunks.append((wkv[c * P:(c + 1) * P, 0:D], wk_s, c))
        for c in range(KC):
            chunks.append((wq[c * P:(c + 1) * P, :], wq_s, c))
        for c in range(CC):
            chunks.append((wkv[c * P:(c + 1) * P, D:2 * D], wv_s, c))
        for c in range(KC):
            chunks.append((wout[c * P:(c + 1) * P, :], wo_s, c))
        assert len(chunks) == W1
        EARLY = CC + KC
        split_before = {"K0": CC, "Q0": EARLY, "V0": EARLY + CC, "O0": W1}

        up_d = up.rearrange("(c p) n -> p c n", p=P)
        ffn_chunks = [("up", m) for m in range(4)]
        for m in range(MC):
            ffn_chunks.append(("dn", m))
            if m + 4 < MC:
                ffn_chunks.append(("up", m + 4))
            if m >= 6 and m < 6 + KC:
                ffn_chunks.append(("ex", m - 6))
        chunk_no = {key: W1 + k for k, key in enumerate(ffn_chunks)}

        tile_at = {(B - 1, 5): 0, (B - 1, 8): 1, (B - 1, 11): 2, (B - 1, 14): 3}
        norm_at = {(i, s - 1): u for (i, s), u in tile_at.items()}
        split_at = {(B - 1, 6): 0, (B - 1, 9): 1, (B - 1, 12): 2, (B - 1, 15): 3,
                    (B, 3): 4, (B, 5): 5, (B, 7): 6, (B, 9): 7}
        ahead_w = len(split_at)

        def planned(plan, i, s):
            return plan.get((i, s)) if isinstance(i, int) else None

        def w_at(m):
            return ffn_chunks[ahead_w + 3 * m:ahead_w + 3 * (m + 1)]

        def ffn_chunk(key):
            kind, m = key
            if kind == "up":
                return up_d[:, :, m * P:(m + 1) * P], [w[:, :, m * P:(m + 1) * P] for w in up_s]
            if kind == "dn":
                return down[m * P:(m + 1) * P, :], [w[:, m, :] for w in dn_s]
            return wexp[m * P:(m + 1) * P, :], [w[:, m, :] for w in ex_s]

        def raw2(k, key):
            r = y_s[:, k % 4, :]
            return r.rearrange("p (c n) -> p c n", c=KC) if key[0] == "up" else r

        def alone(eng):
            eng.sem_inc(passed, 1)

        block = stack.enter_context(nc.Block())

        def phase1(eng, iteration, ahead=0, later_setup=None):
            iteration(-2, 0)
            if later_setup:
                later_setup()
            for i in range(-1, 2):
                iteration(i, i)
            with eng.Fori(0, (B - 4) // 2 - ahead) as trip:
                iteration(2 * trip + 2, 0)
                iteration(2 * trip + 3, 1)
            for i in range(B - 2 - 2 * ahead, B + 1):
                iteration(i, i)

        @block.sync
        def _(sp):
            def load_x(b):
                for t in range(TT):
                    n = b * TT + t
                    if some(n - 1):
                        sp.wait_ge(xn_made, n - 1)
                    alone(sp)
                    sp.dma_start(xin[t][:], xt_d[n]).then_inc(x_in[t], INC)
                if some(b):
                    sp.wait_ge(ctx_split, 2 * b)
                alone(sp)
                sp.dma_start(ctx_raw[:], ctx_d[b]).then_inc(ctx_in, INC)

            def store_turned(b, par):
                if some(b - 1):
                    for half in range(2):
                        sp.wait_ge(st_in[half], INC * STACK_DMAS * (b - 1))
                        alone(sp)
                for dst, src, last_job in zip(qk_d[par], (qT, kT), ("qT1", "kT1")):
                    sp.wait_ge(p_taken, len(PREP_JOBS) * b + PREP_JOBS.index(last_job) + 1)
                    alone(sp)
                    for part in range(2):
                        sp.dma_start(dst[part].rearrange("(c p) s -> p c s", p=P),
                                     src[part][:].bitcast(F32)).then_inc(turned_out[last_job[0]], INC)

            def load_stacks(b, par, half):
                if some((b - 2) * STEPS + 8 * (half + 1)):
                    sp.wait_ge(b_done, (b - 2) * STEPS + 8 * (half + 1))
                    alone(sp)
                slots = slice(8 * half, 8 * half + 8)
                for name, dst, src, parts in (("q", st_q[par], qk_d[par][0], Q_PARTS),
                                              ("k", st_k[par], qk_d[par][1], K_PARTS)):
                    sp.wait_ge(turned_out[name], 2 * INC * (b + 1))
                    alone(sp)
                    for r, part in enumerate(parts):
                        heads = src[part].rearrange("(l q d) s -> q d l s", q=2, d=HD)
                        for q in range(2):
                            row = 64 * q + HD * r
                            sp.dma_start(dst[row:row + HD, slots, :].bitcast(F32),
                                         heads[q, :, slots, :]).then_inc(st_in[half], INC)

            def load_max(b, par, half):
                sp.wait_ge(m_taken, len(MID_JOBS) * b + MID_JOBS.index(f"m{half}") + 1)
                for part in range(2):
                    for q in range(2):
                        row = 64 * q + ROWS_A + part
                        sp.dma_start(st_q[par][row:row + 1, 8 * half:8 * half + 8, :].bitcast(F32),
                                     mT[part][q:NH // 2:2, :].bitcast(F32)).then_inc(m_in, INC)

            def iteration(i, par):
                b2, b1, bt = i + 2, i + 1, i - 1

                def store_x1(t):
                    n = bt * TT + t
                    sp.wait_ge(x1_made, n + 1)
                    alone(sp)
                    sp.dma_start(x1_d[n], xres[t][:]).then_inc(x1_out[t], INC)

                if within(b1):
                    load_stacks(b1, (par + 1) % 2, 1)
                if within(i):
                    load_max(i, par % 2, 1)
                if within(bt):
                    for t in range(TT):
                        n = bt * TT + t
                        if some(bt):
                            sp.wait_ge(x1_out[t], INC * bt)
                        if isinstance(bt, int) and bt == 0:
                            sp.wait_ge(w_lo, W1)
                        alone(sp)
                        sp.dma_start(xres[t][:], xt_d[n]).then_inc(res_in[t], INC)
                    if isinstance(i, int) and i == B - 1:
                        first_loads()
                    if isinstance(i, int) and i == B:
                        for key in ffn_chunks[4:ahead_w]:
                            load_w(key)
                    store_x1(0)
                if within(b1):
                    load_max(b1, (par + 1) % 2, 0)
                if within(i + 3):
                    load_x(i + 3)
                if within(b2):
                    store_turned(b2, par % 2)
                    load_stacks(b2, par % 2, 0)
                if isinstance(i, int) and i == B - 1:
                    load_fx(1)
                    load_fx(2)
                if within(bt):
                    store_x1(1)
                if isinstance(i, int) and i == B - 1:
                    load_fx(3)

            def load_raw(low, high):
                for k in range(low, high):
                    sp.dma_start(raw1[k], chunks[k][0]).then_inc(w_raw[k], INC)

            def load_fx(n):
                if some(n):
                    sp.wait_ge(x_done, x_job(n - 1) + 1)
                alone(sp)
                sp.dma_start(fx[:], x1_d[n]).then_inc(fx_in, INC)

            def x_job(n):
                return (UT + 2) * (n // UT) + n % UT

            def load_w(key):
                k = chunk_no[key]
                if k >= W1 + 4:
                    sp.wait_ge(w_lo, k - 3)
                sp.dma_start(raw2(k, key), ffn_chunk(key)[0]).then_inc(f_raw[k % 4], INC)

            def first_loads():
                sp.wait_ge(b_done, STEPS * (B - 1))
                sp.wait_ge(roped, len(ROPES) * B)
                sp.wait_ge(p_taken, len(PREP_JOBS) * B)
                for x in "qk":
                    sp.wait_ge(turned_out[x], 2 * INC * B)
                sp.wait_ge(m_taken, len(MID_JOBS) * (B - 1) + V_DONE)
                for t in range(TT):
                    sp.wait_ge(x1_out[t], INC * (BLK // S))
                sp.dma_start(g_gamma[:], gamma.partition_broadcast(P)).then_inc(f_small, INC)
                sp.dma_start(g_beta[:], beta.partition_broadcast(P)).then_inc(f_small, INC)
                sp.dma_start(gt_raw[:], gate.rearrange("(c p) e -> p c e", p=P)).then_inc(f_small, INC)
                load_fx(0)
                for key in ffn_chunks[:4]:
                    load_w(key)

            load_raw(0, CC)
            load_x(0)
            sp.dma_start(pos_s, posT).then_inc(pos_in, INC)
            load_raw(CC, EARLY)
            sp.dma_start(g_att[:], g_x.partition_broadcast(P)).then_inc(small_in, INC)
            sp.dma_start(g_ffn[:], g_f.partition_broadcast(P)).then_inc(small_in, INC)
            sp.dma_start(gbout[:], bout.partition_broadcast(P)).then_inc(small_in, INC)
            load_raw(EARLY, W1)
            sp.wait_ge(k_ones, 2)
            phase1(sp, iteration, ahead=1)

            for t in range(TT):
                sp.wait_ge(x1_out[t], INC * B)
            def next_fx(j, u):
                sp.wait_ge(x_done, (UT + 2) * (j + 1) + u if u else (UT + 2) * (j + 1))
                alone(sp)
                sp.dma_start(fx[:], x1_d[(j + 1) * UT + u]).then_inc(fx_in, INC)

            def fblock(j, first_block=False, last=False):
                if not first_block:
                    for u in range(UT):
                        n = (j - 1) * UT + u
                        if u >= 2:
                            sp.wait_ge(out_made, n - 1)
                            alone(sp)
                            sp.dma_start(out_d[n - 2], y_s[:, u - 2, :]).then_inc(out_out[u - 2], INC)
                        sp.dma_start(fres[u % 2][:], x1_d[n]).then_inc(fres_in[u % 2], INC)
                    for u in range(UT - 2, UT):
                        n = (j - 1) * UT + u
                        sp.wait_ge(out_made, n + 1)
                        alone(sp)
                        sp.dma_start(out_d[n], y_s[:, u, :]).then_inc(out_out[u], INC)
                if first_block:
                    for m in range(MC):
                        if m + 2 in X_AT:
                            next_fx(j, X_AT.index(m + 2))
                        for key in w_at(m):
                            load_w(key)
                elif not last:
                    for u in range(UT):
                        next_fx(j, u)

            fblock(0, first_block=True)
            with sp.Fori(0, (NB - 2) // 2) as trip:
                fblock(2 * trip + 1)
                fblock(2 * trip + 2)
            fblock(NB - 1, last=True)
            fblock(NB, last=True)
            for u in range(UT):
                sp.wait_ge(out_out[u], INC * NB)

        @block.gpsimd
        def _(pool):
            nc.gpsimd.memset(ident[:], 0.0).then_inc(ident_made, 1)
            nc.gpsimd.memset(neg_half[:], -0.5)
            for i in range(2):
                last = nc.gpsimd.memset(v_s[i][:, :, :, HD:HD + 1], 1.0)
            last.then_inc(consts_made, 1)
            for i in range(2):
                nc.gpsimd.memset(st_k[i][:].bitcast(F32), 1.0).then_inc(k_ones, 1)
            pool.wait_ge(ident_made, 1)
            nc.gpsimd.affine_select(out=ident[:], in_=ident[:], compare_op=ALU.not_equal, fill=1.0, base=0,
                                    pattern=[[-1, P]], channel_multiplier=1).then_inc(ident_made, 1)

            def inv_std(count):
                pool.wait_ge(mv_made, count)
                if some(count - 1):
                    pool.wait_ge(rstd_made, count - 1)
                alone(pool)
                nc.gpsimd.tensor_scalar_add(var_eps[:], meanvar[:, 1:2], EPS).then_inc(ve_made, 1)
                pool.wait_ge(ve_made, count)
                nc.gpsimd.tensor_tensor(rstd[:], var_eps[:], neg_half[:], ALU.pow).then_inc(rstd_made, 1)

            def rope_sum(b, name):
                r = ROPES.index(name)
                pool.wait_ge(p_taken, len(PREP_JOBS) * b + PREP_JOBS.index(name) + 1)
                t1 = rot[name[0]]
                nc.gpsimd.tensor_tensor(t1[:], t1[:], rot2[:], ALU.add).then_inc(roped, 1)

            def pool_step(b, what):
                if isinstance(what, int):
                    inv_std(b * TT + what + 1)
                else:
                    rope_sum(b, what)

            def split_ctx(b, par):
                pool.wait_ge(ctx_in, INC * (b + 1))
                hi, lo = ctx_s[par]
                if some(b - 1):
                    pool.wait_ge(m_done, len(MID_JOBS) * (b - 2) + V_DONE)
                alone(pool)
                nc.gpsimd.tensor_copy(hi[:], ctx_raw[:]).then_inc(ctx_split, 1)
                pool.wait_ge(ctx_split, 2 * b + 1)
                nc.gpsimd.tensor_tensor(lo[:], ctx_raw[:], hi[:].bitcast(F32), ALU.subtract).then_inc(ctx_split, 1)

            def iteration(i, par):
                b2, bt = i + 2, i - 1
                if within(b2):
                    for what in POOL_ORDER[:3]:
                        pool_step(b2, what)
                if within(bt):
                    if isinstance(i, int) and bt == 0:
                        pool.wait_ge(bias_made, 1)
                    for t in range(TT):
                        pool.wait_ge(res_in[t], INC * (bt + 1))
                        nc.gpsimd.tensor_tensor(xres[t][:], xres[t][:], gbout[:], ALU.add).then_inc(res_made, 1)
                if within(b2):
                    for what in POOL_ORDER[3:]:
                        pool_step(b2, what)
                if within(i + 3):
                    split_ctx(i + 3, (par + 1) % 2)
                if isinstance(i, int) and i == B - 1:
                    for u in range(UT):
                        inv_std(NT + u + 1)

            split_ctx(0, 0)
            phase1(pool, iteration, ahead=1)

            def ffn_inv_std(count):
                inv_std(NT + count)

            def for_output(j, u, count):
                r = fres[u % 2]
                pool.wait_ge(fres_in[u % 2], INC * (2 * j + u // 2 + 1))
                nc.gpsimd.tensor_tensor(r[:], r[:], g_beta[:], ALU.add).then_inc(fres_made, 1)
                ffn_inv_std(count)

            pool.wait_ge(gb_made, 2)

            def fblock(j, first_block=False, last=False):
                done = 2 * UT * j
                if not first_block:
                    for u in range(UT):
                        for_output(j - 1, u, done + u + 1)
                if not last:
                    for u in range(UT):
                        ffn_inv_std(done + UT + u + 1)

            fblock(0, first_block=True)
            with pool.Fori(0, (NB - 2) // 2) as trip:
                fblock(2 * trip + 1)
                fblock(2 * trip + 2)
            fblock(NB - 1, last=True)
            for u in range(UT):
                for_output(NB - 1, u, 2 * UT * NB - UT + u + 1)

        @block.scalar
        def _(act):
            def round_weights(low, high):
                for k in range(low, high):
                    act.wait_ge(w_raw[k], INC)
                    nc.scalar.copy(chunks[k][1][0][:, chunks[k][2], :], raw1[k]).then_inc(w_hi, 1)

            round_weights(0, CC)
            act.wait_ge(setup, 8)
            nc.scalar.activation(sin_a, ang.rearrange("p n a j -> p n (a j)"), ACT.Sin).then_inc(trig, 1)
            nc.scalar.activation(cos_a, turns.rearrange("p n a j -> p n (a j)"), ACT.Sin).then_inc(trig, 1)
            round_weights(CC, EARLY)

            def later_setup():
                act.wait_ge(small_in, INC * 3)
                nc.scalar.activation(g_att[:], g_att[:], ACT.Tanh).then_inc(gates_made, 1)
                nc.scalar.activation(g_ffn[:], g_ffn[:], ACT.Tanh).then_inc(gates_made, 1)
                round_weights(EARLY, W1)

            def job(kind, name, i, par):
                if kind == "p":
                    b, par = i + 2, par % 2
                    if not within(b) or name not in PREP_SPLITS:
                        return
                    act.wait_ge(p_done, len(PREP_JOBS) * b + PREP_JOBS.index(name) + 1)
                    psum = pP[:, :].rearrange("p (c s) -> p c s", c=KC)
                    t = int(name[-1])
                    if name[0] == "X":
                        nc.scalar.copy(xnT[0][:], psum).then_inc(p_hi, 1)
                        return
                    if some(b):
                        act.wait_ge(turned_out[name[0]], 2 * INC * b)
                    if name[0] == "q":
                        nc.scalar.mul(qT[0][:, :, t * P:(t + 1) * P], psum, SCALE).then_inc(p_hi, 1)
                    else:
                        nc.scalar.copy(kT[0][:, :, t * P:(t + 1) * P], psum).then_inc(p_hi, 1)
                elif kind in "mn":
                    b = i + 1 if kind == "m" else i
                    par = (par + 1) % 2 if kind == "m" else par % 2
                    if not within(b):
                        return
                    act.wait_ge(m_done, len(MID_JOBS) * b + MID_JOBS.index(name) + 1)
                    k = int(name[-1])
                    if name[0] == "V":
                        if some(b - 1):
                            act.wait_ge(av_done, GROUPS * (b - 1))
                        nc.scalar.copy(v_s[par][:, k, :, 0:HD],
                                       pM[:, :].rearrange("p (h e) -> p h e", h=NH)).then_inc(m_taken, 1)
                    else:
                        if some(2 * b + k):
                            act.wait_ge(m_in, 4 * INC * (2 * b + k))
                        nc.scalar.copy(mT[0][:], pM[0:NH // 2, 0:S]).then_inc(m_hi, 1)
                else:
                    b = i - 1 if kind == "t" else i
                    if not within(b) or name[:2] != "aT":
                        return
                    act.wait_ge(t_done, len(TAIL_JOBS) * b + TAIL_JOBS.index(name) + 1)
                    nc.scalar.copy(aT[0][:], pT[:, :].rearrange("p (c s) -> p c s", c=KC)).then_inc(t_hi, 1)

            def take_av(b, g):
                act.wait_ge(av_done, GROUPS * b + g + 1)
                need = len(TAIL_JOBS) * (b - 1) + (2 if g < GROUPS // 2 else 4)
                if some(need):
                    act.wait_ge(t_done, need)
                nc.scalar.copy(av_s[:, g, :], pO[:, 0:S]).then_inc(av_taken, 1)

            def split(key):
                k = chunk_no[key]
                act.wait_ge(f_raw[k % 4], INC * ((k - W1) // 4 + 1))
                nc.scalar.copy(ffn_chunk(key)[1][0], raw2(k, key)).then_inc(w_hi, 1)

            def turned(j, par, u):
                act.wait_ge(x_done, (UT + 2) * j + u + 1)
                nc.scalar.copy(fT[par][0][:, :, u * P:(u + 1) * P],
                               pX.rearrange("p (c s) -> p c s", c=KC)).then_inc(x_hi, 1)

            def iteration(i, par):
                for s in range(STEPS):
                    for item in SLOTS.get((s, 0), []):
                        if item[-1] != "<":
                            job(item[0], item[2:], i, par)
                    if within(i):
                        if isinstance(i, int) and i == 0 and s == 0:
                            act.wait_ge(w_lo, W1)
                        act.wait_ge(b_done, STEPS * i + s + 1)
                        if some(GROUPS * i + s // 2 - 1):
                            act.wait_ge(av_done, GROUPS * i + s // 2 - 1)
                        nc.scalar.activation(probs[:, s % 4, :, :, :].rearrange("p a b s -> p a (b s)"),
                                             pB[:, :, :], ACT.Exp).then_inc(exp_done, 1)
                    if s % 2 and s > 1 and within(i):
                        take_av(i, s // 2 - 1)
                    elif s == 1 and within(i - 1):
                        take_av(i - 1, GROUPS - 1)
                    for item in SLOTS.get((s, 1), []):
                        if item[-1] != "<":
                            job(item[0], item[2:], i, par)
                    if planned(tile_at, i, s) is not None:
                        turned(0, 0, planned(tile_at, i, s))
                    if planned(split_at, i, s) is not None:
                        split(ffn_chunks[planned(split_at, i, s)])
                    if isinstance(i, int) and i == B and s == 2:
                        act.wait_ge(av_done, GROUPS * B)
                if isinstance(i, int) and i == B - 1:
                    act.wait_ge(f_small, 3 * INC)
                    nc.scalar.copy(gt_s[0][:], gt_raw[:]).then_inc(gt_hi, 1)

            phase1(act, iteration, later_setup=later_setup)

            for t in range(TT):
                act.wait_ge(x1_out[t], INC * B)

            def fblock(j, par, first_block=False, last=False):
                for m in range(MC):
                    a = MC * j + m
                    act.wait_ge(u_done, a + 1)
                    if some(a - 1):
                        act.wait_ge(hid_lo, a - 1)
                    nc.scalar.activation(relu[m % 2][:], pU[m % 2], ACT.Relu).then_inc(relu_made, 1)
                    act.wait_ge(relu_made, a + 1)
                    if m >= 2:
                        act.wait_ge(d_done, (MC - 2) * j + m - 1)
                    elif some(UT * j):
                        act.wait_ge(tile_done, UT * j)
                    nc.scalar.activation(hid[m % 2][0][:], relu[m % 2][:], ACT.Square).then_inc(hid_hi, 1)
                    if m == 1:
                        act.wait_ge(x_done, (UT + 2) * j + UT + 1)
                        nc.scalar.copy(gl, pX[0:NEXP, :]).then_inc(x_taken, 1)
                    if not last and m in X_AT:
                        turned(j + 1, (par + 1) % 2, X_AT.index(m))
                    if m in E_AT:
                        u = E_AT.index(m)
                        expert_out(j, par, u)
                    if first_block:
                        for key in w_at(m):
                            split(key)

            def expert_out(j, par, u):
                act.wait_ge(e_done, UT * j + u + 1)
                act.wait_ge(route_made, j + 1)
                if isinstance(j, int) and j == 0:
                    act.wait_ge(w_lo, W1 + len(ffn_chunks))
                else:
                    act.wait_ge(out_out[u], INC * j)
                nc.scalar.activation(y_s[:, u, :], pE, ACT.Copy,
                                     scale=route[par % 2][:, u:u + 1]).then_inc(e_taken, 1)

            fblock(0, 0, first_block=True)
            with act.Fori(0, (NB - 2) // 2) as trip:
                fblock(2 * trip + 1, 1)
                fblock(2 * trip + 2, 0)
            fblock(NB - 1, 1, last=True)

        @block.tensor
        def _(pe):
            pe.wait_ge(ident_made, 2)
            pe.wait_ge(o_zeroed, 1)
            pe.wait_ge(consts_made, 1)

            def product(dst, lhs, rhs, chunks_, half=None):
                low = chunks_ // 2 if half == 1 else 0
                high = chunks_ // 2 if half == 0 else chunks_
                for c in range(low, high):
                    for a, w in PASSES:
                        last = nc.tensor.matmul(dst, lhs(a, c), rhs(w, c), start=(c == 0 and (a, w) == PASSES[0]),
                                                stop=(c == chunks_ - 1 and (a, w) == PASSES[-1]))
                return last

            def turn(dst, src):
                for c in range(KC):
                    last = nc.tensor.transpose(dst[:, c * P:(c + 1) * P], src(c), ident[:])
                return last

            def job(kind, name, i, par):
                if isinstance(i, int) and i == {"p": -2, "m": -1, "t": 1}.get(kind) and name.rstrip("<") in split_before and (
                        name[-1] == "<" or name not in CUT):
                    pe.wait_ge(w_lo, split_before[name.rstrip("<")])
                name, half = (name[:-1], 0) if name[-1] == "<" else (name, 1 if name in CUT else None)
                if kind == "p":
                    b, par = i + 2, par % 2
                    if not within(b):
                        return
                    pos = PREP_JOBS.index(name)
                    if half != 1 and some(len(PREP_JOBS) * b + pos):
                        pe.wait_ge(p_taken, len(PREP_JOBS) * b + pos)
                    t = int(name[-1])
                    if name[0] == "X":
                        pe.wait_ge(xn_made, TT * b + t + 1)
                        last = turn(pP, lambda c: xn[:, c * P:(c + 1) * P])
                    elif name[0] == "Q":
                        last = product(pP[:, :], lambda a, c: xnT[a][:, c, :], lambda w, c: wq_s[w][:, c, :], KC,
                                       half)
                    elif name[0] == "K":
                        if half != 1:
                            pe.wait_ge(ctx_split, 2 * b + 2)
                        last = product(pP[:, :], lambda a, c: ctx_s[par][a][:, c, t * P:(t + 1) * P],
                                       lambda w, c: wk_s[w][:, c, :], CC, half)
                    else:
                        src = rot[name[0].upper()]
                        pe.wait_ge(roped, len(ROPES) * b + ROPES.index(name[0].upper() + name[-1]) + 1)
                        last = turn(pP, lambda c: src[:, c * P:(c + 1) * P])
                    if half != 0:
                        last.then_inc(p_done, 1)
                elif kind in "mn":
                    b = i + 1 if kind == "m" else i
                    par = (par + 1) % 2 if kind == "m" else par % 2
                    if not within(b):
                        return
                    pos = MID_JOBS.index(name)
                    k = int(name[-1])
                    if half != 1 and some(len(MID_JOBS) * b + pos):
                        pe.wait_ge(m_taken, len(MID_JOBS) * b + pos)
                    if name[0] == "V":
                        last = product(pM[:, :], lambda a, c: ctx_s[par][a][:, c, k * P:(k + 1) * P],
                                       lambda w, c: wv_s[w][:, c, :], CC, half)
                    else:
                        pe.wait_ge(max_done, STEPS * b + 8 * (k + 1))
                        for t in range(TT):
                            last = nc.tensor.transpose(pM[0:NH // 2, t * P:(t + 1) * P],
                                                       mneg[par][:, t, k * 16:(k + 1) * 16], ident[:])
                    if half != 0:
                        last.then_inc(m_done, 1)
                else:
                    b = i - 1 if kind == "t" else i
                    if not within(b):
                        return
                    pos = TAIL_JOBS.index(name)
                    if half != 1 and some(len(TAIL_JOBS) * b + pos):
                        pe.wait_ge(t_taken, len(TAIL_JOBS) * b + pos)
                    if name[:2] == "aT":
                        last = turn(pT, lambda c: attn[int(name[-1])][:, c * P:(c + 1) * P])
                    elif name[0] == "O":
                        last = product(pT[:, :], lambda a, c: aT[a][:, c, :], lambda w, c: wo_s[w][:, c, :], KC,
                                       half)
                    else:
                        t, heads = int(name[1]), int(name[2])
                        pe.wait_ge(av_taken, GROUPS * b + GROUPS // 2 * (heads + 1))
                        last = turn(pT, lambda c: av_s[:, GROUPS // 2 * heads + c, t * P:(t + 1) * P])
                    if half != 0:
                        last.then_inc(t_done, 1)

            def logits_a(b, par, s):
                if s % 8 == 0:
                    pe.wait_ge(st_in[s // 8], INC * STACK_DMAS * (b + 1))
                if some(STEPS * b + s):
                    pe.wait_ge(max_done, STEPS * b + s)
                for t in range(TT):
                    for q in range(2):
                        rows = slice(64 * q, 64 * q + ROWS_A)
                        last = nc.tensor.matmul(pA[:, q, t * S:(t + 1) * S], st_q[par][rows, s, t * P:(t + 1) * P],
                                                st_k[par][rows, s, :], start=True, stop=True)
                last.then_inc(a_done, 1)

            def logits_b(b, par, s):
                if s % 8 == 0:
                    pe.wait_ge(m_in, 4 * INC * (2 * b + s // 8 + 1))
                if some(STEPS * b + s):
                    pe.wait_ge(exp_done, STEPS * b + s)
                for t in range(TT):
                    for q in range(2):
                        rows = slice(64 * q, 64 * q + ROWS_B)
                        last = nc.tensor.matmul(pB[:, q, t * S:(t + 1) * S], st_k[par][rows, s, t * P:(t + 1) * P],
                                                st_q[par][rows, s, :], start=True, stop=True)
                last.then_inc(b_done, 1)

            def times_v(b, par, g, t):
                if t == 0:
                    pe.wait_ge(exp_done, STEPS * b + 2 * g + 2)
                    if g == 0:
                        pe.wait_ge(m_taken, len(MID_JOBS) * b + V_DONE)
                    if some(GROUPS * b + g):
                        pe.wait_ge(av_taken, GROUPS * b + g)
                for j in range(4):
                    last = nc.tensor.matmul(pO[32 * j:32 * j + HD + 1, 0:S], v_s[par][:, t, 4 * g + j, :],
                                            probs[:, (2 * g + j // 2) % 4, j % 2, t, :],
                                            start=(t == 0), stop=(t == TT - 1))
                if t == TT - 1:
                    last.then_inc(av_done, 1)

            def turned(j, u):
                n = UT * j + u
                pe.wait_ge(fxn_made, n + 1)
                if isinstance(j, int) and j == 0 and u == 0:
                    pe.wait_ge(m_taken, len(MID_JOBS) * B)
                if some((UT + 2) * j + u):
                    pe.wait_ge(x_taken, (UT + 2) * j + u)
                turn(pX, lambda c: fx[:, c * P:(c + 1) * P]).then_inc(x_done, 1)

            def iteration(i, par):
                for s in range(STEPS):
                    if within(i + 1):
                        for k in maxima_steps(i, s):
                            logits_a(i + 1, (par + 1) % 2, k)
                    for item in SLOTS.get((s, 0), []):
                        job(item[0], item[2:], i, par)
                    if within(i):
                        logits_b(i, par % 2, s)
                    if s >= 2 and within(i):
                        times_v(i, par % 2, s // 2 - 1, s % 2)
                    elif s < 2 and within(i - 1):
                        times_v(i - 1, (par + 1) % 2, GROUPS - 1, s)
                    for item in SLOTS.get((s, 1), []):
                        job(item[0], item[2:], i, par)
                    if planned(tile_at, i, s) is not None:
                        turned(0, planned(tile_at, i, s))

            phase1(pe, iteration)

            def routing(j, par):
                pe.wait_ge(x_taken, (UT + 2) * j + UT)
                product(pX[0:NEXP, :], lambda a, c: gt_s[a][:, c, :], lambda w, c: fT[par][w][:, c, :],
                        KC).then_inc(x_done, 1)

            def routing_turned(j):
                pe.wait_ge(x_taken, (UT + 2) * j + UT + 1)
                alone(pe)
                for u in range(UT):
                    last = nc.tensor.transpose(pX[:, u * NEXP:(u + 1) * NEXP], gl[:, u * P:(u + 1) * P],
                                               ident[0:NEXP, 0:NEXP])
                last.then_inc(x_done, 1)

            def hidden(j, par, m, first_block):
                a = MC * j + m
                if some(a - 1):
                    pe.wait_ge(relu_made, a - 1)
                if m == 0:
                    pe.wait_ge(x_taken, (UT + 2) * j + UT)
                if first_block:
                    pe.wait_ge(w_lo, chunk_no["up", m] + 1)
                product(pU[m % 2], lambda x_, c: up_s[x_][:, c, m * P:(m + 1) * P],
                        lambda w, c: fT[par][w][:, c, :], KC).then_inc(u_done, 1)

            def shared(j, chunks_, first_block):
                pe.wait_ge(hid_lo, MC * j + chunks_[-1] + 1)
                if chunks_[0] == 0 and some(UT * j):
                    pe.wait_ge(y_made, UT * j)
                if first_block:
                    pe.wait_ge(w_lo, chunk_no["dn", chunks_[-1]] + 1)
                for u in range(UT):
                    for m in chunks_:
                        for k, (x_, w) in enumerate(PASSES):
                            last = nc.tensor.matmul(acc[u], hid[m % 2][x_][:, u * P:(u + 1) * P], dn_s[w][:, m, :],
                                                    start=(m == 0 and k == 0), stop=(m == MC - 1 and k == 2))
                    if m == MC - 1:
                        last.then_inc(tile_done, 1)
                if m < MC - 1:
                    last.then_inc(d_done, 1)

            def expert(j, par, u, first_block):
                if first_block:
                    pe.wait_ge(w_lo, chunk_no["ex", KC - 1] + 1)
                if first_block and u == 0:
                    pe.wait_ge(t_taken, len(TAIL_JOBS) * B)
                if some(UT * j + u):
                    pe.wait_ge(e_taken, UT * j + u)
                product(pE, lambda a, c: fT[par][a][:, c, u * P:(u + 1) * P], lambda w, c: ex_s[w][:, c, :],
                        KC).then_inc(e_done, 1)

            def fblock(j, par, first_block=False, last=False):
                for m in range(MC):
                    hidden(j, par, m, first_block)
                    if m == 0:
                        routing(j, par)
                    if m == 2:
                        routing_turned(j)
                    if 1 <= m < MC - 1:
                        shared(j, (m - 1,), first_block)
                    if not last and m in X_AT:
                        turned(j + 1, X_AT.index(m))
                    if m in E_AT:
                        expert(j, par, E_AT.index(m), first_block)
                shared(j, (MC - 2, MC - 1), first_block)

            pe.wait_ge(gt_lo, 1)
            pe.wait_ge(p_taken, len(PREP_JOBS) * B)
            fblock(0, 0, first_block=True)
            with pe.Fori(0, (NB - 2) // 2) as trip:
                fblock(2 * trip + 1, 1)
                fblock(2 * trip + 2, 0)
            fblock(NB - 1, 1, last=True)

        @block.vector
        def _(dve):
            nc.vector.memset(pO[:, :], 0.0).then_inc(o_zeroed, 1)

            def split_weights(low, high):
                for k in range(low, high):
                    dve.wait_ge(w_hi, k + 1)
                    _, dst, c = chunks[k]
                    nc.vector.tensor_tensor(dst[1][:, c, :], raw1[k], dst[0][:, c, :].bitcast(F32),
                                            ALU.subtract).then_inc(w_lo, 1)

            def later_setup():
                split_weights(EARLY, W1)
                dve.wait_ge(gates_made, 2)
                nc.vector.tensor_scalar(gbout[:], gbout[:], g_att[:, 0:1], None, ALU.mult).then_inc(bias_made, 1)

            dve.wait_ge(pos_in, INC)
            for j in range(HALF):
                freq = float(np.float32(ROPE_BASE ** (-j / HALF)))
                last = nc.vector.tensor_scalar(ang[:, :, :, j], pos_s, freq, None, ALU.mult)
            last.then_inc(setup, 1)
            two_pi = 2.0 * float(np.pi)
            hi_pi = float(np.float32(two_pi))
            round_to = 1.5 * 2.0 ** 23
            dve.wait_ge(setup, 1)
            nc.vector.tensor_scalar(turns, ang, 1.0 / two_pi, round_to, ALU.mult, ALU.add).then_inc(setup, 1)
            dve.wait_ge(setup, 2)
            nc.vector.tensor_scalar(turns, turns, -round_to, None, ALU.add).then_inc(setup, 1)
            for k, part in enumerate((hi_pi, two_pi - hi_pi)):
                dve.wait_ge(setup, 3 + k)
                nc.vector.scalar_tensor_tensor(ang, turns, -part, ang, ALU.mult, ALU.add).then_inc(setup, 1)
            dve.wait_ge(setup, 5)
            pi = float(np.float32(3.1415925))
            nc.vector.tensor_scalar(ang, ang, pi, -pi, ALU.min, ALU.max).then_inc(setup, 1)
            dve.wait_ge(setup, 6)
            nc.vector.scalar_tensor_tensor(turns, ang, -1.0, ang, ALU.mult, ALU.min).then_inc(setup, 1)
            dve.wait_ge(setup, 7)
            nc.vector.tensor_scalar(turns, turns, float(np.pi) / 2, None, ALU.add).then_inc(setup, 1)
            split_weights(0, CC)
            dve.wait_ge(trig, 2)
            nc.vector.tensor_copy(cos_t[:, :, :, 0], cos_a)
            nc.vector.tensor_copy(cos_t[:, :, :, 1], cos_a)
            nc.vector.tensor_copy(sin_t[:, :, :, 1], sin_a)
            nc.vector.tensor_scalar(sin_t[:, :, :, 0], sin_a, -1.0, None, ALU.mult).then_inc(tables, 1)
            split_weights(CC, EARLY)
            dve.wait_ge(tables, 1)

            def mean_var(src, count):
                if some(count - 1):
                    dve.wait_ge(mv_made, count - 1)
                nc.vector.bn_stats(stats[:], src).then_inc(st_made, 1)
                dve.wait_ge(st_made, count)
                if some(count - 1):
                    dve.wait_ge(rstd_made, count - 1)
                alone(dve)
                nc.vector.bn_aggr(meanvar[:], stats[:]).then_inc(mv_made, 1)

            def normalise(dst, src, count):
                dve.wait_ge(rstd_made, count)
                return nc.vector.tensor_scalar(dst, src, meanvar[:, 0:1], rstd[:, 0:1], ALU.subtract, ALU.mult)

            def job(kind, name, i, par):
                if kind == "p":
                    b = i + 2
                    if not within(b):
                        return
                    pos = PREP_JOBS.index(name)
                    t = int(name[-1])
                    if name in PREP_SPLITS:
                        dve.wait_ge(p_hi, len(PREP_SPLITS) * b + PREP_SPLITS.index(name) + 1)
                        psum = pP[:, :].rearrange("p (c s) -> p c s", c=KC)
                        if name[0] == "X":
                            op = nc.vector.tensor_tensor(xnT[1][:], psum, xnT[0][:].bitcast(F32), ALU.subtract)
                        else:
                            src, scale = (qT, SCALE) if name[0] == "q" else (kT, 1.0)
                            cut = slice(t * P, (t + 1) * P)
                            op = nc.vector.scalar_tensor_tensor(src[1][:, :, cut], psum, scale,
                                                                src[0][:, :, cut].bitcast(F32),
                                                                ALU.mult, ALU.subtract)
                        op.then_inc(p_taken, 1)
                        return
                    dve.wait_ge(p_done, len(PREP_JOBS) * b + pos + 1)
                    n = TT * b + t
                    xv = pP[:, :].rearrange("p (h k two) -> p h k two", h=NH, two=2)
                    r = ROPES.index(name)

                    def table(a):
                        return a[:, bass.ds(n, 1), :, :].to_broadcast([P, NH, ANG, 2])

                    def view(a):
                        return a[:].rearrange("p (h k two) -> p h k two", h=NH, two=2)

                    nc.vector.tensor_tensor(view(rot[name[0]]), xv, table(cos_t), ALU.mult)
                    if some(len(ROPES) * b + r):
                        dve.wait_ge(roped, len(ROPES) * b + r)
                    nc.vector.tensor_tensor(view(rot2), xv[:, :, :, ::-1], table(sin_t), ALU.mult).then_inc(p_taken, 1)
                elif kind in "mn":
                    b = i + 1 if kind == "m" else i
                    if not within(b) or name[0] == "V":
                        return
                    dve.wait_ge(m_hi, 2 * b + int(name[-1]) + 1)
                    nc.vector.tensor_tensor(mT[1][:], pM[0:NH // 2, 0:S], mT[0][:].bitcast(F32),
                                            ALU.subtract).then_inc(m_taken, 1)
                else:
                    b = i - 1 if kind == "t" else i
                    if not within(b):
                        return
                    pos = TAIL_JOBS.index(name)
                    t = int(name[-1]) if name[0] != "a" or name[1] == "T" else int(name[1])
                    if name[:2] == "aT":
                        dve.wait_ge(t_hi, TT * b + t + 1)
                        nc.vector.tensor_tensor(aT[1][:], pT[:, :].rearrange("p (c s) -> p c s", c=KC),
                                                aT[0][:].bitcast(F32), ALU.subtract).then_inc(t_taken, 1)
                        return
                    dve.wait_ge(t_done, len(TAIL_JOBS) * b + pos + 1)
                    if name[0] == "O":
                        n = TT * b + t
                        dve.wait_ge(res_made, n + 1)
                        nc.vector.scalar_tensor_tensor(xres[t][:], pT[:, :], g_att[:, 0:1], xres[t][:],
                                                       ALU.mult, ALU.add).then_inc(x1_made, 1)
                        dve.wait_ge(x1_made, n + 1)
                        nc.vector.nop().then_inc(t_taken, 1)
                        return
                    half = int(name[2])
                    heads = pT[:, :].rearrange("p (h e) -> p h e", e=32)
                    c = 4 * b + pos
                    nc.vector.reciprocal(rden[:], heads[:, :, HD]).then_inc(rd_made, 1)
                    dve.wait_ge(rd_made, c + 1)
                    nc.vector.tensor_tensor(
                        attn[t][:, half * D // 2:(half + 1) * D // 2].rearrange("p (h e) -> p h e", e=HD),
                        heads[:, :, 0:HD], rden[:].unsqueeze(2).to_broadcast([P, NH // 2, HD]),
                        ALU.mult).then_inc(t_taken, 1)

            def split(key):
                k = chunk_no[key]
                dve.wait_ge(w_hi, k + 1)
                hi, lo = ffn_chunk(key)[1]
                nc.vector.tensor_tensor(lo, raw2(k, key), hi.bitcast(F32), ALU.subtract).then_inc(w_lo, 1)

            def norm_in(n, count):
                dve.wait_ge(fx_in, INC * (n + 1))
                mean_var(fx[:], NT + count)
                normalise(fx[:], fx[:], NT + count).then_inc(fxn_made, 1)

            def turned(j, par, u):
                dve.wait_ge(x_hi, UT * j + u + 1)
                cut = slice(u * P, (u + 1) * P)
                nc.vector.tensor_tensor(fT[par][1][:, :, cut], pX.rearrange("p (c s) -> p c s", c=KC),
                                        fT[par][0][:, :, cut].bitcast(F32), ALU.subtract).then_inc(x_taken, 1)

            def scale_affine():
                dve.wait_ge(f_small, 3 * INC)
                nc.vector.tensor_scalar(g_gamma[:], g_gamma[:], g_ffn[:, 0:1], None, ALU.mult).then_inc(gb_made, 1)
                nc.vector.tensor_scalar(g_beta[:], g_beta[:], g_ffn[:, 0:1], None, ALU.mult).then_inc(gb_made, 1)
                dve.wait_ge(gt_hi, 1)
                nc.vector.tensor_tensor(gt_s[1][:], gt_raw[:], gt_s[0][:].bitcast(F32), ALU.subtract).then_inc(gt_lo, 1)

            def iteration(i, par):
                for s in range(STEPS):
                    if within(i + 2):
                        for t, at in enumerate(LN_AT):
                            n = TT * (i + 2) + t
                            if s == at:
                                dve.wait_ge(x_in[t], INC * (i + 3))
                                mean_var(xin[t][:], n + 1)
                            if s == at + 1:
                                if some(n):
                                    before = len(PREP_JOBS) * (i + 1 + t) + PREP_JOBS.index(f"X{1 - t}") + 1
                                    dve.wait_ge(p_done, before)
                                normalise(xn[:], xin[t][:], n + 1).then_inc(xn_made, 1)
                    if within(i + 1):
                        b = i + 1
                        for k in maxima_steps(i, s):
                            dve.wait_ge(a_done, STEPS * b + k + 1)
                            nc.vector.tensor_reduce(
                                mneg[(par + 1) % 2][:, :, 2 * k:2 * k + 2].rearrange("p t q -> p q t"),
                                pA[:, :, :].rearrange("p q (t k) -> p q t k", t=TT), AX.X, ALU.max,
                                negate=True).then_inc(max_done, 1)
                    for slot in range(2):
                        for item in SLOTS.get((s, slot), []):
                            if item[-1] != "<":
                                job(item[0], item[2:], i, par)

                    if isinstance(i, int) and i == B and s == 2:
                        dve.wait_ge(av_done, GROUPS * B)
                    if planned(norm_at, i, s) is not None:
                        norm_in(planned(norm_at, i, s), planned(norm_at, i, s) + 1)
                    if planned(tile_at, i, s) is not None:
                        turned(0, 0, planned(tile_at, i, s))
                    if planned(split_at, i, s) is not None:
                        split(ffn_chunks[planned(split_at, i, s)])
                if isinstance(i, int) and i == B - 1:
                    scale_affine()

            phase1(dve, iteration, later_setup=later_setup)

            for t in range(TT):
                dve.wait_ge(x1_out[t], INC * B)
            def sum_y(j, tiles=range(UT)):
                for u in tiles:
                    dve.wait_ge(tile_done, UT * j + u + 1)
                    dve.wait_ge(e_taken, UT * j + u + 1)
                    nc.vector.tensor_tensor(y_s[:, u, :], acc[u], y_s[:, u, :], ALU.add).then_inc(y_made, 1)

            def norm_y(j, u, count):
                n = UT * j + u
                y = y_s[:, u, :]
                dve.wait_ge(y_made, n + 1)
                mean_var(y, NT + count)
                dve.wait_ge(mv_made, NT + count)
                nc.vector.scalar_tensor_tensor(y, y, meanvar[:, 0:1], g_gamma[:], ALU.subtract,
                                               ALU.mult).then_inc(z_made, 1)
                dve.wait_ge(z_made, n + 1)
                dve.wait_ge(rstd_made, NT + count)
                dve.wait_ge(fres_made, n + 1)
                nc.vector.scalar_tensor_tensor(y, y, rstd[:, 0:1], fres[u % 2][:], ALU.mult,
                                               ALU.add).then_inc(out_made, 1)

            def fblock(j, par, first_block=False, last=False):
                done = 2 * UT * j
                if not first_block:
                    sum_y(j - 1)
                for m in range(MC):
                    a = MC * j + m
                    r = relu[m % 2]
                    dve.wait_ge(hid_hi, a + 1)
                    nc.vector.tensor_tensor(r[:], r[:], r[:], ALU.mult).then_inc(sq_made, 1)
                    dve.wait_ge(sq_made, a + 1)
                    nc.vector.tensor_tensor(hid[m % 2][1][:], r[:], hid[m % 2][0][:].bitcast(F32),
                                            ALU.subtract).then_inc(hid_lo, 1)
                    if m == 3:
                        dve.wait_ge(x_done, (UT + 2) * j + UT + 2)
                        nc.vector.tensor_copy(glT[:], pX[:, 0:UT * NEXP].rearrange("p (u e) -> p u e", u=UT)
                                              ).then_inc(x_taken, 1)
                        dve.wait_ge(x_taken, (UT + 2) * j + UT + 2)
                        alone(dve)
                        for u in range(UT):
                            last_op = nc.vector.max(top[:, u, :], glT[:, u, :])
                        last_op.then_inc(top_made, 1)
                        dve.wait_ge(top_made, j + 1)
                        nc.vector.tensor_tensor(route[par % 2][:], top[:, :, 0], top[:, :, 1],
                                                ALU.add).then_inc(route_made, 1)
                    if not first_block and m < UT:
                        norm_y(j - 1, m, done + m + 1)
                    if not last and m + 1 in X_AT:
                        u = X_AT.index(m + 1)
                        norm_in(UT * (j + 1) + u, done + UT + u + 1)
                    if not last and m in X_AT:
                        turned(j + 1, (par + 1) % 2, X_AT.index(m))
                    if first_block:
                        for key in w_at(m):
                            split(key)

            fblock(0, 0, first_block=True)
            with dve.Fori(0, (NB - 2) // 2) as trip:
                fblock(2 * trip + 1, 1)
                fblock(2 * trip + 2, 0)
            fblock(NB - 1, 1, last=True)
            for u in range(UT):
                sum_y(NB - 1, [u])
                norm_y(NB - 1, u, 2 * UT * NB - UT + u + 1)


def kernel(**inputs):
    import concourse.bacc as bacc
    from concourse.bass_utils import run_bass_kernel_spmd

    a = {k: np.asarray(v) for k, v in inputs.items()}
    pos = a["fside_BxSx2_0"].reshape(NT, P, POS)
    arrays = {
        "x": a["x"],
        "ctxT": a["ctx_1024"].transpose(0, 2, 1),
        "posT": pos.transpose(1, 0, 2),
        "g_x": a["g_xattn"],
        "g_f": a["g_ffn"],
        "wq": a["L0_xattn_Wq"],
        "wkv": a["L0_xattn_Wkv"],
        "wout": a["L0_xattn_Wout"],
        "bout": a["L0_xattn_bout"],
        "gate": a["L0_ffn_gate_w"],
        "up": a["L0_ffn_up_w"],
        "down": a["L0_ffn_down_w"],
        "wexp": a["L0_ffn_expert_weight"],
        "gamma": a["L0_ffn_ln_gamma"],
        "beta": a["L0_ffn_ln_beta"],
    }
    arrays = {k: np.ascontiguousarray(v) for k, v in arrays.items()}
    nc = bacc.Bacc("TRN2", target_bir_lowering=False, num_devices=1)
    args = [nc.dram_tensor(k, v.shape, mybir.dt.from_np(v.dtype), kind="ExternalInput").ap()
            for k, v in arrays.items()]
    out = nc.dram_tensor("out", (B, S, D), F32, kind="ExternalOutput").ap()
    flamingo_gated(nc, *args, out)
    r = run_bass_kernel_spmd(nc, [arrays], core_ids=[0])
    return r.results[0]["out"]
```
